# Optimizing a Trainium2 kernel written in Bass

```python
import numpy as np
import jax
import jax.numpy as jnp

def _softmax(x, axis=-1):
    return jax.nn.softmax(x, axis=axis)

def _gelu(x):
    return jax.nn.gelu(x, approximate=True)

def _silu(x):
    return jax.nn.silu(x)

def _sigmoid(x):
    return jax.nn.sigmoid(x)

def _layernorm(x, axis=-1, eps=1e-05):
    m = jnp.mean(x, axis=axis, keepdims=True)
    v = jnp.var(x, axis=axis, keepdims=True)
    return (x - m) / jnp.sqrt(v + eps)

def _scatter_add(tgt, idx, src, axis=0):
    return tgt.at[idx].add(src)

def _segment_sum(src, seg, n):
    return jax.ops.segment_sum(src, seg, n)
kernel_name = 'mk_audio_tower_d1_tok_audfeat768_r4_3a4d3a'

def setup_inputs(seed: int=0):
    np.random.seed(seed)
    _w = jnp.asarray

    def _rec_inputs():
        import jax
        import jax.numpy as jnp
        _rk = jax.random.key(seed)
        x = -0.000222058 + 0.999998 * jax.random.normal(jax.random.fold_in(_rk, 1), (8, 750, 192), jnp.float32)
        return x
    x = _rec_inputs()

    def _L0_tok_setup():
        import jax, jax.numpy as jnp
        import numpy as np
        B, S, D, K = (8, 1024, 192, 7)
        EPS = 1e-05
        key = jax.random.key(seed)
        k0, k1, k2, k3, k4 = jax.random.split(key, 5)
        return {'x': jax.random.normal(k0, (B, S, D), jnp.float32), 'w_dw': jax.random.normal(k1, (D, 1, K), jnp.float32) * 0.2, 'b_dw': jax.random.normal(k2, (D,), jnp.float32) * 0.02, 'w_pw': jax.random.normal(k3, (D, D, 1), jnp.float32) * 0.03, 'b_pw': jax.random.normal(k4, (D,), jnp.float32) * 0.02, 'gamma': jnp.ones((D,), jnp.float32), 'beta': jnp.zeros((D,), jnp.float32)}
    _L0_tok_all = _L0_tok_setup()
    _L0_tok_in = {k: v for k, v in _L0_tok_all.items() if k in ('w_dw', 'b_dw', 'w_pw', 'b_pw', 'gamma', 'beta')}
    del _L0_tok_all

    def _L0_attn_setup():
        import jax, jax.numpy as jnp
        import numpy as np
        B, N, D = (4, 2048, 192)
        H, DH = (12, 64)
        INNER = H * DH
        key = jax.random.key(seed)
        k0, k1, k2 = jax.random.split(key, 3)
        return {'x': jax.random.normal(k0, (B, N, D), dtype=jnp.float32), 'w_qkv': jax.random.normal(k1, (D, INNER), dtype=jnp.float32) * 0.02, 'temp': jnp.ones((H, 1), dtype=jnp.float32), 'w_out': jax.random.normal(k2, (INNER, D), dtype=jnp.float32) * 0.02, 'b_out': jnp.zeros((D,), dtype=jnp.float32)}
    _L0_attn_all = _L0_attn_setup()
    _L0_attn_in = {k: v for k, v in _L0_attn_all.items() if k in ('w_qkv', 'temp', 'w_out', 'b_out')}
    del _L0_attn_all

    def _L0_ffn_setup():
        import jax, jax.numpy as jnp
        import numpy as np
        B, L, D, H, F = (4, 512, 192, 12, 768)
        ROUTE_FRAC = 0.15
        LN_EPS = 1e-05

        def _ln(x, g, b):
            m = jnp.mean(x, axis=-1, keepdims=True)
            v = jnp.mean((x - m) ** 2, axis=-1, keepdims=True)
            return (x - m) * jax.lax.rsqrt(v + LN_EPS) * g + b
        key = jax.random.key(seed)
        ks = jax.random.split(key, 20)
        s = 0.02
        return {'hidden_states': jax.random.normal(ks[0], (B, L, D), dtype=jnp.float32), 'g1': jnp.ones((D,), jnp.float32), 'b1': jnp.zeros((D,), jnp.float32), 'g2': jnp.ones((D,), jnp.float32), 'b2': jnp.zeros((D,), jnp.float32), 'Wr': jax.random.normal(ks[1], (D,), jnp.float32) * s, 'br': jnp.zeros((), jnp.float32), 'Wq': jax.random.normal(ks[2], (D, D), jnp.float32) * s, 'bq': jnp.zeros((D,), jnp.float32), 'Wk': jax.random.normal(ks[3], (D, D), jnp.float32) * s, 'bk': jnp.zeros((D,), jnp.float32), 'Wv': jax.random.normal(ks[4], (D, D), jnp.float32) * s, 'bv': jnp.zeros((D,), jnp.float32), 'Wo': jax.random.normal(ks[5], (D, D), jnp.float32) * s, 'bo': jnp.zeros((D,), jnp.float32), 'Wm': jax.random.normal(ks[6], (D, D), jnp.float32) * s, 'bm': jnp.zeros((D,), jnp.float32), 'W1': jax.random.normal(ks[7], (D, F), jnp.float32) * s, 'bf1': jnp.zeros((F,), jnp.float32), 'W2': jax.random.normal(ks[8], (F, D), jnp.float32) * s, 'bf2': jnp.zeros((D,), jnp.float32)}
    _L0_ffn_all = _L0_ffn_setup()
    _L0_ffn_in = {k: v for k, v in _L0_ffn_all.items() if k in ('g1', 'b1', 'g2', 'b2', 'Wr', 'br', 'Wq', 'bq', 'Wk', 'bk', 'Wv', 'bv', 'Wo', 'bo', 'Wm', 'bm', 'W1', 'bf1', 'W2', 'bf2')}
    del _L0_ffn_all
    return {'x': x, 'L0_tok_w_dw': _L0_tok_in['w_dw'], 'L0_tok_b_dw': _L0_tok_in['b_dw'], 'L0_tok_w_pw': _L0_tok_in['w_pw'], 'L0_tok_b_pw': _L0_tok_in['b_pw'], 'L0_tok_gamma': _L0_tok_in['gamma'], 'L0_tok_beta': _L0_tok_in['beta'], 'L0_attn_w_qkv': _L0_attn_in['w_qkv'], 'L0_attn_temp': _L0_attn_in['temp'], 'L0_attn_w_out': _L0_attn_in['w_out'], 'L0_attn_b_out': _L0_attn_in['b_out'], 'L0_ffn_g1': _L0_ffn_in['g1'], 'L0_ffn_b1': _L0_ffn_in['b1'], 'L0_ffn_g2': _L0_ffn_in['g2'], 'L0_ffn_b2': _L0_ffn_in['b2'], 'L0_ffn_Wr': _L0_ffn_in['Wr'], 'L0_ffn_br': _L0_ffn_in['br'], 'L0_ffn_Wq': _L0_ffn_in['Wq'], 'L0_ffn_bq': _L0_ffn_in['bq'], 'L0_ffn_Wk': _L0_ffn_in['Wk'], 'L0_ffn_bk': _L0_ffn_in['bk'], 'L0_ffn_Wv': _L0_ffn_in['Wv'], 'L0_ffn_bv': _L0_ffn_in['bv'], 'L0_ffn_Wo': _L0_ffn_in['Wo'], 'L0_ffn_bo': _L0_ffn_in['bo'], 'L0_ffn_Wm': _L0_ffn_in['Wm'], 'L0_ffn_bm': _L0_ffn_in['bm'], 'L0_ffn_W1': _L0_ffn_in['W1'], 'L0_ffn_bf1': _L0_ffn_in['bf1'], 'L0_ffn_W2': _L0_ffn_in['W2'], 'L0_ffn_bf2': _L0_ffn_in['bf2']}

def reference(x, L0_tok_w_dw, L0_tok_b_dw, L0_tok_w_pw, L0_tok_b_pw, L0_tok_gamma, L0_tok_beta, L0_attn_w_qkv, L0_attn_temp, L0_attn_w_out, L0_attn_b_out, L0_ffn_g1, L0_ffn_b1, L0_ffn_g2, L0_ffn_b2, L0_ffn_Wr, L0_ffn_br, L0_ffn_Wq, L0_ffn_bq, L0_ffn_Wk, L0_ffn_bk, L0_ffn_Wv, L0_ffn_bv, L0_ffn_Wo, L0_ffn_bo, L0_ffn_Wm, L0_ffn_bm, L0_ffn_W1, L0_ffn_bf1, L0_ffn_W2, L0_ffn_bf2):
    import jax
    import jax.numpy as jnp

    def _L0_tok_ref(x, w_dw, b_dw, w_pw, b_pw, gamma, beta):
        import jax, jax.numpy as jnp
        import numpy as np
        B, S, D, K = (8, 1024, 192, 7)
        EPS = 1e-05
        d = w_dw.shape[0]
        h = jnp.transpose(x, (0, 2, 1))
        h = jax.lax.conv_general_dilated(h, w_dw, window_strides=(1,), padding='SAME', dimension_numbers=('NCH', 'OIH', 'NCH'), feature_group_count=d) + b_dw[None, :, None]
        h = jnp.einsum('od,bds->bos', w_pw[:, :, 0], h) + b_pw[None, :, None]
        h = jax.nn.relu(h)
        h = jax.lax.reduce_window(h, -jnp.inf, jax.lax.max, (1, 1, 2), (1, 1, 2), 'VALID')
        h = jnp.transpose(h, (0, 2, 1))
        y = jnp.real(jnp.fft.fft2(h))
        mu = jnp.mean(y, axis=-1, keepdims=True)
        var = jnp.var(y, axis=-1, keepdims=True)
        return (y - mu) * jax.lax.rsqrt(var + EPS) * gamma + beta

    def _L0_attn_ref(x, w_qkv, temp, w_out, b_out):
        import jax, jax.numpy as jnp
        import numpy as np
        B, N, D = (4, 2048, 192)
        H, DH = (12, 64)
        INNER = H * DH
        b, n, _ = x.shape
        h = temp.shape[0]
        w = (x @ w_qkv).reshape(b, n, h, -1).transpose(0, 2, 1, 3)
        norm = jnp.sqrt(jnp.sum(w * w, axis=2, keepdims=True))
        w_normed = w / jnp.maximum(norm, 1e-12)
        logits = jnp.sum(w_normed * w_normed, axis=-1) * temp
        Pi = jax.nn.softmax(logits, axis=-1)
        Pi_norm = Pi / (jnp.sum(Pi, axis=-1, keepdims=True) + 1e-08)
        dots = jnp.einsum('bhn,bhnd->bhd', Pi_norm, w * w)[:, :, None, :]
        attn = 1.0 / (1.0 + dots)
        out = -(w * Pi[..., None]) * attn
        out = out.transpose(0, 2, 1, 3).reshape(b, n, -1)
        return out @ w_out + b_out

    def _L0_ffn_ref(hidden_states, g1, b1, g2, b2, Wr, br, Wq, bq, Wk, bk, Wv, bv, Wo, bo, Wm, bm, W1, bf1, W2, bf2):
        import jax, jax.numpy as jnp
        import numpy as np
        B, L, D, H, F = (4, 512, 192, 12, 768)
        ROUTE_FRAC = 0.15
        LN_EPS = 1e-05

        def _ln(x, g, b):
            m = jnp.mean(x, axis=-1, keepdims=True)
            v = jnp.mean((x - m) ** 2, axis=-1, keepdims=True)
            return (x - m) * jax.lax.rsqrt(v + LN_EPS) * g + b
        b, l, d = hidden_states.shape
        dh = d // H
        normed = _ln(hidden_states, g1, b1)
        scores = jax.nn.sigmoid(jnp.einsum('bld,d->bl', normed, Wr) + br)
        k = max(1, int(round(ROUTE_FRAC * l)))
        _, idx = jax.lax.top_k(-scores, k)
        attn_mask = jnp.zeros((b, l), bool).at[jnp.arange(b)[:, None], idx].set(True)
        q = (normed @ Wq + bq).reshape(b, l, H, dh)
        kk = (normed @ Wk + bk).reshape(b, l, H, dh)
        v = (normed @ Wv + bv).reshape(b, l, H, dh)
        logits = jnp.einsum('blhd,bmhd->bhlm', q, kk) / jnp.sqrt(jnp.float32(dh))
        probs = jax.nn.softmax(logits, axis=-1)
        ctx = jnp.einsum('bhlm,bmhd->blhd', probs, v).reshape(b, l, d)
        attn_out = ctx @ Wo + bo
        w = scores / (jnp.sum(scores, axis=1, keepdims=True) + 1e-06)
        pooled = jnp.einsum('bl,bld->bd', w, normed)
        mix_out = (normed + scores[..., None] * pooled[:, None, :]) @ Wm + bm
        merged = jnp.where(attn_mask[..., None], attn_out, mix_out)
        h = hidden_states + merged
        n2 = _ln(h, g2, b2)
        ffn = jax.nn.gelu(n2 @ W1 + bf1, approximate=False) @ W2 + bf2
        return h + ffn
    h = _L0_tok_ref(x, L0_tok_w_dw, L0_tok_b_dw, L0_tok_w_pw, L0_tok_b_pw, L0_tok_gamma, L0_tok_beta)
    h = h + _L0_attn_ref(_layernorm(h, axis=-1), L0_attn_w_qkv, L0_attn_temp, L0_attn_w_out, L0_attn_b_out)
    h = h + _L0_ffn_ref(_layernorm(h, axis=-1), L0_ffn_g1, L0_ffn_b1, L0_ffn_g2, L0_ffn_b2, L0_ffn_Wr, L0_ffn_br, L0_ffn_Wq, L0_ffn_bq, L0_ffn_Wk, L0_ffn_bk, L0_ffn_Wv, L0_ffn_bv, L0_ffn_Wo, L0_ffn_bo, L0_ffn_Wm, L0_ffn_bm, L0_ffn_W1, L0_ffn_bf1, L0_ffn_W2, L0_ffn_bf2)
    return h

_drawn_inputs = setup_inputs


def setup_inputs(seed=0):
    import zlib

    import numpy as np

    out = dict(_drawn_inputs(seed))
    spreads = {'L0_tok_gamma': (1.0, 0.2),
     'L0_tok_beta': (0.0, 0.1),
     'L0_attn_temp': (1.0, 0.6),
     'L0_attn_b_out': (0.0, 0.1),
     'L0_ffn_g1': (1.0, 0.2),
     'L0_ffn_b1': (0.0, 0.429),
     'L0_ffn_g2': (1.0, 0.6),
     'L0_ffn_b2': (0.0, 2.0),
     'L0_ffn_bq': (0.0, 0.8),
     'L0_ffn_bk': (0.0, 2.0),
     'L0_ffn_bv': (0.0, 0.8),
     'L0_ffn_bo': (0.0, 0.413),
     'L0_ffn_bm': (0.0, 0.1),
     'L0_ffn_bf1': (0.0, 0.529),
     'L0_ffn_bf2': (0.0, 0.1)}
    factors = {'L0_attn_w_qkv': 8.0,
     'L0_attn_w_out': 8.0,
     'L0_ffn_Wq': 8.0,
     'L0_ffn_Wk': 8.0,
     'L0_ffn_Wv': 8.0,
     'L0_ffn_Wo': 8.0}
    for name, (base, spread) in spreads.items():
        noise = np.random.default_rng([zlib.crc32(name.encode()), seed]).standard_normal(out[name].shape)
        drawn = base * np.exp(spread * noise) if base else spread * noise
        out[name] = jnp.asarray(drawn.astype(out[name].dtype))
    for name, factor in factors.items():
        out[name] = (out[name] * factor).astype(out[name].dtype)
    return out
```

```python
import concourse.bass as bass
from concourse import mybir
from contextlib import ExitStack

B, S, D, K = 8, 750, 192, 7
N = S // 2
P, T = 125, 3
C, CT = 96, 2
H1, IT = 12, 6
KF = N // 2 + 1
NE = N + 1
SEL = int(round(0.15 * N))
Q = 64
EPS = 1e-5


class Signal:

    def __init__(self, sem, per_batch):
        self.sem, self.per_batch = sem, per_batch

    def of(self, b, j=None):
        return self.sem, b * self.per_batch + (self.per_batch if j is None else j)

    def before(self, b, j=None):
        j = self.per_batch if j is None else j
        return self.sem, b * self.per_batch + (j - self.per_batch)


def audio_tower(nc, dram, out):
    fp32, bf16 = mybir.dt.float32, mybir.dt.bfloat16
    ALU, ACT, AX = mybir.AluOpType, mybir.ActivationFunctionType, mybir.AxisListType

    with ExitStack() as ctx:
        def sb(name, shape, dt=fp32):
            return ctx.enter_context(nc.sbuf_tensor(name, shape, dt))

        def signal(name, per_batch=1):
            return Signal(ctx.enter_context(nc.semaphore(name)), per_batch)

        x_in = sb("x_in", [C, CT, S + 6])
        w_dw = sb("w_dw_sb", [C, CT, K + 1])
        w_pw = sb("w_pw_sb", [C + 1, CT, D])
        dft_n = sb("dft_n_sb", [P, T, 2 * KF])
        dft_d = sb("dft_d_sb", [C, 2, CT, D])
        ident = sb("ident_sb", [128, 128])
        rows = sb("rows_sb", [P, 8, D])
        w_qkv = sb("w_qkv_sb", [C, CT, IT * 128])
        temp = sb("temp_sb", [H1, 1])
        head_mask = sb("head_mask_sb", [128, IT, H1])
        head_sel = sb("head_sel_sb", [96, IT, 128], bf16)
        w_out = sb("w_out_sb", [128, IT, D])
        w_k = sb("w_k_sb", [C, CT, D])
        b_k = sb("b_k_sb", [C, CT])
        w_v = sb("w_v_sb", [C + 1, CT, D + 1])
        w_q = sb("w_q_sb", [C + 1, CT, D])
        w_o = sb("w_o_sb", [C + 1, CT, D])
        w_m = sb("w_m_sb", [C + 1, CT, D])
        q_mask = sb("q_mask_sb", [C, H1 // 2])
        later = sb("later_sb", [P, T, N])
        slot = sb("slot_sb", [Q, 1])
        w_1 = sb("w_1_sb", [C, CT, IT * 128])
        b_1 = sb("b_1_sb", [128, IT])
        w_2 = sb("w_2_sb", [128, IT, D])
        eps3 = sb("eps3", [P, T])
        half3 = sb("half3", [P, T])
        ones = sb("ones", [P, C])
        gate_p = sb("gate_p", [1, 1])
        ones_bf = sb("ones_bf", [P, Q], bf16)

        hid = sb("hid", [P, B, T, D])
        zed = sb("zed", [P, T, D])
        n2T = sb("n2T", [C, B, CT, NE])

        dw = sb("dw", [C + 1, CT, S])
        even = sb("even", [P, T, D])
        pooled_h = sb("pooled_h", [P, T, D])
        fc = sb("fc", [C, CT, NE])
        fs = sb("fs", [C, CT, NE])
        xh = sb("xh", [P, T, D])
        xhT = sb("xhT", [C, CT, NE])

        def norm_buffers(n):
            return (sb(f"st{n}", [P, T, 6]), sb(f"ag{n}", [P, T, 2]), sb(f"ve{n}", [P, T]), sb(f"rs{n}", [P, T]),
                    sb(f"gate{n}", [1, 1]))

        ln1, ln2, ln3, ln5 = (norm_buffers(n) for n in (1, 2, 3, 5))

        w_s = sb("w_s", [128, IT, NE])
        w_sq = sb("w_sq", [128, IT, NE])
        nrm = sb("nrm", [128, IT])
        rnrm = sb("rnrm", [128, IT])
        rhead = sb("rhead", [128, IT, H1])
        lg = sb("lg", [H1, NE])
        lgm = sb("lgm", [H1, 4])
        pi = sb("pi", [H1, NE])
        pi_r = sb("pi_r", [H1, NE])
        pi_mid = sb("pi_mid", [H1, NE], bf16)
        pi_parts = sb("pi_parts", [96, NE], bf16)
        u = w_sq
        junk = sb("junk", [128, NE])
        dots = sb("dots", [128, IT])
        natt = sb("natt", [128, IT])
        w_oa = sb("w_oa", [128, IT, D])
        r3 = sb("r3", [P, T])
        r4a = sb("r4a", [P, T])
        r4b = sb("r4b", [P, T])
        r4c = sb("r4c", [P, T])
        r4 = sb("r4", [P, T])

        nr = sb("nr", [P, T, D + 1])
        nT = sb("nT", [C + 1, CT, NE])
        kT = sb("kT", [C, CT, NE])
        v = sb("v", [P, T, D])
        sexp = sb("sexp", [P, T])
        eqm = sb("eqm", [P, T, NE], bf16)
        less = eqm
        putT = sb("putT", [Q, NE])
        put = sb("put", [P, T, Q])
        pl_s = sb("pl_s", [C, 1])
        pl_r = sb("pl_r", [C, 1])
        pl = sb("pl", [C, CT])
        nsT = sb("nsT", [C + 1, CT, Q])
        msel = sb("msel", [Q, D])
        qb = sb("qb", [C, CT, H1 // 2, Q])
        nmax = sb("nmax", [128, IT])
        psum_p = sb("psum_p", [128, IT])
        rsum_p = sb("rsum_p", [128, IT])
        probs = sb("probs", [128, IT, NE])
        head_sel32 = probs[0:96, :, 0:128]
        probsT = sb("probsT", [P, IT, T, 128])
        cx = sb("cx", [Q, D])
        cxT = sb("cxT", [C + 1, CT, Q])
        att = sb("att", [Q, D])
        n2 = sb("n2", [P, T, D])
        h2 = sb("h2", [P, T, D])

        gelu = [w_s, probs]
        y_out = probsT[:, 0:4, :, :].rearrange("p j t q -> p (j t q)")[:, 0:2 * T * D].rearrange("p (k t d) -> p k t d", k=2, d=D)

        xb = ctx.enter_context(nc.psum_tensor("xb", [128, 2, 512], fp32))
        yb = ctx.enter_context(nc.psum_tensor("yb", [128, 2, 512], fp32))
        zb = ctx.enter_context(nc.psum_tensor("zb", [128, 4, 512], fp32))

        first_in = signal("first_in", 16)
        x_ready = signal("x_ready", 16)
        fft_in = signal("fft_in", 16)
        rest_in = signal("rest_in", 16)
        consts = signal("consts")
        dw_done = signal("dw_done", CT * (K))
        pw_ready, relu_done, pool_done = signal("pw_ready", T), signal("relu_done", T), signal("pool_done", T)
        fa_ready, fcs_done = signal("fa_ready"), signal("fcs_done")
        y_ready = signal("y_ready", 2)
        bn1, ag1, ve1, rs1 = signal("bn1"), signal("ag1"), signal("ve1"), signal("rs1")
        lnt_done, h0_done = signal("lnt_done", T), signal("h0_done", T)
        bn2, ag2, ve2, rs2 = signal("bn2"), signal("ag2"), signal("ve2"), signal("rs2")
        xh_done, xhT_ready, xhT_done = signal("xh_done", T), signal("xhT_ready"), signal("xhT_done")
        qkv_ready, sq_done = signal("qkv_ready", IT), signal("sq_done", IT)
        rn1, rn2, rhead_done = signal("rn1"), signal("rn2"), signal("rhead_done")
        lg_ready, lg_done, lmax_done, lexp_done = signal("lg_ready"), signal("lg_done"), signal("lmax_done"), signal("lexp_done")
        pi_steps, pi_mid0, pi_mid_sig, pi_low_done = signal("pi_steps", 7), signal("pi_mid"), signal("pi_mid_done"), signal("pi_low_done")
        pib_ready, u_done, dots_done = signal("pib_ready", IT), signal("u_done", IT), signal("dots_done", IT)
        att_steps, woa_done = signal("att_steps", 3), signal("woa_done")
        o_ready = signal("o_ready", 2)
        hb_done, h1_done = signal("hb_done"), signal("h1_done", 2)
        bn3, ag3, r_steps = signal("bn3"), signal("ag3"), signal("r_steps", 7)
        z_done, nrt_done, nr_done = signal("z_done", T), signal("nrt_done", T), signal("nr_done", T)
        nT_ready, nT_done, sc_row_done = signal("nT_ready"), signal("nT_done"), signal("sc_row_done")
        k_ready, kT_done = signal("k_ready"), signal("kT_done")
        v_ready, v_done, sexp_done = signal("v_ready", 2), signal("v_done", 2), signal("sexp_done", 2)
        sc_steps = signal("sc_steps", 2)
        sb_ready, less_done, eq_done = signal("sb_ready"), signal("less_done", T), signal("eq_done", T)
        rk_ready, putT_done = signal("rk_ready"), signal("putT_done")
        put_ready, put_done = signal("put_ready"), signal("put_done")
        pl_ready, pl_steps, pwm_ready, pwm_done = signal("pl_ready"), signal("pl_steps", 3), signal("pwm_ready"), signal("pwm_done")
        ns_ready, ns_done = signal("ns_ready"), signal("ns_done")
        q_ready, qb_done = signal("q_ready"), signal("qb_done")
        ms_ready, ms_done = signal("ms_ready"), signal("ms_done")
        ql_ready, qmax_done, prob_done = signal("ql_ready", IT), signal("qmax_done", IT), signal("prob_done", IT)
        prT_ready, prT_done = signal("prT_ready", IT), signal("prT_done", IT)
        pv_ready, rsum_done, cx_done = signal("pv_ready"), signal("rsum_done"), signal("cx_done")
        cxT_ready, cxT_done = signal("cxT_ready"), signal("cxT_done")
        ao_ready, att_done = signal("ao_ready"), signal("att_done")
        mix_ready, h2_done = signal("mix_ready", 2), signal("h2_done", 2)
        hz_done, h12_done = signal("hz_done"), signal("h12_done")
        bn5, ag5, ve5, rs5 = signal("bn5"), signal("ag5"), signal("ve5"), signal("rs5")
        n2t_done, n2_done = signal("n2t_done", T), signal("n2_done", T)
        n2T_ready, n2T_done = signal("n2T_ready"), signal("n2T_done")
        w1_ready, gelu_done = signal("w1_ready", IT), signal("gelu_done", IT)
        w2_ready, y_done, stored = signal("w2_ready", 2), signal("y_done", 2), signal("stored", 16)

        block = ctx.enter_context(nc.Block())

        def tok(t):
            return slice(P * t, P * (t + 1))

        def chan(c):
            return slice(C * c, C * (c + 1))

        firsts = [(w_dw, "w_dw"), (w_pw, "w_pw"), (dw[C:C + 1, 0, :], "ones_row")]
        ffts = [(dft_n, "dft_n"), (dft_d, "dft_d"), (rows, "rows"), (ident, "ident"), (w_qkv, "w_qkv")]
        rests = [(temp, "temp"), (head_mask, "head_mask"), (head_sel32, "head_sel"), (w_out, "w_out"), (w_k, "w_k"),
                 (b_k, "b_k"), (w_v, "w_v"), (w_q, "w_q"), (w_o, "w_o"), (w_m, "w_m"), (q_mask, "q_mask"),
                 (later, "later"), (slot, "slot"), (w_1, "w_1"), (b_1, "b_1"), (w_2, "w_2"),
                 (nT[C:C + 1, 0, 0:N], "ones_n"), (nsT[C:C + 1, 0, :], "ones_q"), (cxT[C:C + 1, 0, :], "ones_q2")]
        FIRST, FFT, REST = (16 * len(x) for x in (firsts, ffts, rests))

        def batches(eng, body):
            body(0)
            with eng.Fori(1, B) as b:
                body(b)

        def first(b):
            return isinstance(b, int) and b == 0

        @block.sync
        def _(sp):
            for dst, name in firsts:
                sp.dma_start(dst if isinstance(dst, bass.AP) else dst[:], dram[name]).then_inc(first_in.sem, 16)
            sp.dma_start(x_in[:], dram["x"][0]).then_inc(x_ready.sem, 16)
            for dst, name in ffts:
                sp.dma_start(dst[:], dram[name]).then_inc(fft_in.sem, 16)
            with sp.Fori(1, B) as b:
                sp.wait_ge(*dw_done.before(b))
                sp.dma_start(x_in[:], dram["x"][b]).then_inc(x_ready.sem, 16)

            def store(b, k):
                done, ring = y_done.of(b)[1], stored.before(b)[1]
                if not first(b):
                    done, ring = (v if isinstance(v, int) else sp.snap(v) for v in (done, ring))
                    sp.wait_ge(stored.sem, ring)
                sp.wait_ge(y_done.sem, done)
                sp.wait_ge(first_in.sem, FIRST)
                sp.dma_start(out[b].rearrange("(t p) d -> p t d", p=P), y_out[:, k]).then_inc(stored.sem, 16)

            store(0, 0)
            store(1, 1)
            with sp.Fori(1, B // 2) as pair:
                store(2 * pair, 0)
                store(2 * pair + 1, 1)
            sp.wait_ge(stored.sem, 16 * B)

        @block.vector
        def _(dve):
            dve.memset(ones[:], 1.0).then_inc(consts.sem, 1)
            dve.memset(ones_bf[:], 1.0).then_inc(consts.sem, 1)
            dve.memset(w_s[:, :, N:NE], 1.0).then_inc(consts.sem, 1)
            dve.memset(pi_parts[:], 0.0).then_inc(consts.sem, 1)
            dve.wait_ge(first_in.sem, FIRST)

            def norm(b, src, buffers, bn, ag):
                st, agg, _, _, gate = buffers
                dve.memset(gate[:], 0.0)
                for t in range(T):
                    ins = dve.bn_stats(st[:, t, :], src(t))
                ins.then_inc(bn.sem, 1)
                dve.wait_ge(*bn.of(b))
                dve.memset(gate[:], 0.0)
                for t in range(T):
                    ins = dve.bn_aggr(agg[:, t, :], st[:, t, :])
                ins.then_inc(ag.sem, 1)

            def depthwise(b):
                dve.wait_ge(*x_ready.of(b))
                if not first(b):
                    dve.wait_ge(*pw_ready.before(b))
                for k in range(K):
                    for c in range(CT):
                        src = x_in[:, c, k:k + S]
                        if k == 0:
                            ins = dve.tensor_scalar(dw[0:C, c, :], src, w_dw[:, c, 0:1], w_dw[:, c, K:K + 1], ALU.mult, ALU.add)
                        else:
                            dve.wait_ge(*dw_done.of(b, CT * (k - 1) + c + 1))
                            ins = dve.scalar_tensor_tensor(out=dw[0:C, c, :], in0=src, scalar=w_dw[:, c, k:k + 1],
                                                           in1=dw[0:C, c, :], op0=ALU.mult, op1=ALU.add)
                        ins.then_inc(dw_done.sem, 1)

            def pool_pairs(b):
                if not first(b):
                    dve.wait_ge(*fa_ready.before(b))
                for t in range(T):
                    dve.wait_ge(*relu_done.of(b, t + 1))
                    dve.scalar_tensor_tensor(out=pooled_h[:, t, :], in0=xb[0:P, t % 2, D:2 * D], scalar=0.0, in1=even[:, t, :],
                                             op0=ALU.max, op1=ALU.max).then_inc(pool_done.sem, 1)

            def spectrum_norm(b):
                def y(t):
                    return xb[0:P, t // 2, D * (t % 2):D * (t % 2) + D]
                if b is not None:
                    dve.wait_ge(*y_ready.of(b))
                norm(b, y, ln1, bn1, ag1)
                dve.wait_ge(*ag1.of(b))
                if first(b):
                    dve.wait_ge(fft_in.sem, FFT)
                for t in range(T):
                    dve.scalar_tensor_tensor(out=hid[:, b, t, :], in0=y(t), scalar=ln1[1][:, t, 0:1], in1=rows[:, 0, :],
                                             op0=ALU.subtract, op1=ALU.mult).then_inc(lnt_done.sem, 1)
                dve.wait_ge(*rs1.of(b))
                dve.wait_ge(*lnt_done.of(b))
                for t in range(T):
                    dve.scalar_tensor_tensor(out=hid[:, b, t, :], in0=hid[:, b, t, :], scalar=ln1[3][:, t:t + 1], in1=rows[:, 1, :],
                                             op0=ALU.mult, op1=ALU.add).then_inc(h0_done.sem, 1)

            def second_norm(b):
                dve.wait_ge(*h0_done.of(b))
                norm(b, lambda t: hid[:, b, t, :], ln2, bn2, ag2)
                dve.wait_ge(*ag2.of(b))
                dve.wait_ge(*rs2.of(b))
                if not first(b):
                    dve.wait_ge(*xhT_ready.before(b))
                for t in range(T):
                    dve.tensor_scalar(xh[:, t, :], hid[:, b, t, :], ln2[1][:, t, 0:1], ln2[3][:, t:t + 1],
                                      ALU.subtract, ALU.mult).then_inc(xh_done.sem, 1)

            def token_norms(b):
                dve.wait_ge(*sq_done.of(b))
                dve.tensor_scalar(nrm[:], nrm[:], 1e-24, None, ALU.max).then_inc(rn1.sem, 1)
                dve.wait_ge(*rn1.of(b))
                dve.reciprocal(rnrm[:], nrm[:]).then_inc(rn2.sem, 1)
                dve.wait_ge(*rn2.of(b))
                dve.tensor_tensor(rhead[:], head_mask[:], rnrm[:].unsqueeze(2).to_broadcast([128, IT, H1]), ALU.mult)\
                   .then_inc(rhead_done.sem, 1)

            def token_softmax(b):
                dve.wait_ge(*lg_ready.of(b))
                dve.tensor_scalar(lg[:, 0:N], yb[0:H1, 0, 0:N], temp[:], None, ALU.mult).then_inc(lg_done.sem, 1)
                dve.wait_ge(*lg_done.of(b))
                dve.tensor_reduce(lgm[:, 0:1], lg[:, 0:N], AX.X, ALU.max, negate=True).then_inc(lmax_done.sem, 1)
                dve.wait_ge(*lexp_done.of(b))
                dve.reciprocal(lgm[:, 2:3], lgm[:, 1:2]).then_inc(pi_steps.sem, 1)
                dve.wait_ge(*pi_steps.of(b, 1))
                dve.tensor_scalar(pi[:, 0:N], lg[:, 0:N], lgm[:, 2:3], None, ALU.mult).then_inc(pi_steps.sem, 1)
                dve.wait_ge(*pi_steps.of(b, 2))
                dve.tensor_reduce(lgm[:, 3:4], pi[:, 0:N], AX.X, ALU.add).then_inc(pi_steps.sem, 1)
                dve.wait_ge(*pi_steps.of(b, 3))
                dve.tensor_scalar(lgm[:, 3:4], lgm[:, 3:4], 1e-8, None, ALU.add).then_inc(pi_steps.sem, 1)
                dve.wait_ge(*pi_steps.of(b, 4))
                dve.reciprocal(pi[:, N:NE], lgm[:, 3:4]).then_inc(pi_steps.sem, 1)
                dve.wait_ge(*pi_steps.of(b, 5))
                if not first(b):
                    dve.wait_ge(*pib_ready.before(b))
                dve.tensor_copy(pi_parts[0:H1, :], pi[:]).then_inc(pi_steps.sem, 1)
                dve.wait_ge(*pi_steps.of(b, 6))
                dve.tensor_tensor(pi_r[:], pi[:], pi_parts[0:H1, :], ALU.subtract).then_inc(pi_steps.sem, 1)
                dve.wait_ge(*pi_mid_sig.of(b))
                dve.tensor_tensor(pi_parts[64:64 + H1, :], pi_r[:], pi_mid[:], ALU.subtract).then_inc(pi_low_done.sem, 1)

            def token_products(b):
                for j in range(IT):
                    dve.wait_ge(*pib_ready.of(b, j + 1))
                    dve.tensor_tensor(u[:, j, :], w_s[:, j, :], yb[:, j % 2, 0:NE], ALU.mult).then_inc(u_done.sem, 1)
                    dve.wait_ge(*u_done.of(b, j + 1))
                    dve.tensor_tensor_reduce(out=junk[:, 0:N], in0=u[:, j, 0:N], in1=w_s[:, j, 0:N], scale=1.0, scalar=0.0,
                                             op0=ALU.mult, op1=ALU.add, accum_out=dots[:, j:j + 1]).then_inc(dots_done.sem, 1)
                dve.wait_ge(*dots_done.of(b))
                dve.tensor_tensor(natt[:], dots[:], u[:, :, N], ALU.mult).then_inc(att_steps.sem, 1)
                dve.wait_ge(*att_steps.of(b, 1))
                dve.tensor_scalar(natt[:], natt[:], -1.0, -1.0, ALU.mult, ALU.add).then_inc(att_steps.sem, 1)
                dve.wait_ge(*att_steps.of(b, 2))
                dve.reciprocal(natt[:], natt[:]).then_inc(att_steps.sem, 1)
                dve.wait_ge(*att_steps.of(b, 3))
                dve.tensor_tensor(w_oa[:], w_out[:], natt[:].unsqueeze(2).to_broadcast([128, IT, D]), ALU.mult)\
                   .then_inc(woa_done.sem, 1)

            def third_norm(b):
                dve.wait_ge(*hb_done.of(b))
                for k, (t0, t1) in enumerate(((0, 2), (2, 3))):
                    dve.wait_ge(*o_ready.of(b, k + 1))
                    dve.tensor_tensor(hid[:, b, t0:t1, :], yb[0:P, k, 0:D * (t1 - t0)].rearrange("p (t d) -> p t d", d=D),
                                      hid[:, b, t0:t1, :], ALU.add).then_inc(h1_done.sem, 1)
                dve.wait_ge(*h1_done.of(b))
                norm(b, lambda t: hid[:, b, t, :], ln3, bn3, ag3)
                dve.wait_ge(*r_steps.of(b, 2))
                if not first(b):
                    dve.wait_ge(*h2_done.before(b))
                for t in range(T):
                    dve.tensor_scalar(zed[:, t, :], hid[:, b, t, :], ln3[1][:, t, 0:1], r3[:, t:t + 1],
                                      ALU.subtract, ALU.mult).then_inc(z_done.sem, 1)
                if not first(b):
                    dve.wait_ge(*ns_ready.before(b))
                for t in range(T):
                    dve.scalar_tensor_tensor(out=nr[:, t, 0:D], in0=hid[:, b, t, :], scalar=ln3[1][:, t, 0:1], in1=rows[:, 3, :],
                                             op0=ALU.subtract, op1=ALU.mult).then_inc(nrt_done.sem, 1)
                dve.wait_ge(*r_steps.of(b))
                for t in range(T):
                    dve.wait_ge(*nrt_done.of(b, t + 1))
                    dve.scalar_tensor_tensor(out=nr[:, t, 0:D], in0=nr[:, t, 0:D], scalar=r4[:, t:t + 1], in1=rows[:, 4, :],
                                             op0=ALU.mult, op1=ALU.add).then_inc(nr_done.sem, 1)

            def route(b):
                dve.wait_ge(*sexp_done.of(b))
                dve.tensor_scalar(sexp[:], sexp[:], 1.0, None, ALU.add).then_inc(sc_steps.sem, 1)
                dve.wait_ge(*sc_steps.of(b, 1))
                dve.reciprocal(nr[:, :, D], sexp[:]).then_inc(sc_steps.sem, 1)
                dve.wait_ge(*sb_ready.of(b))
                if not first(b):
                    dve.wait_ge(*rk_ready.before(b))
                for t in range(T):
                    dve.scalar_tensor_tensor(out=eqm[:, t, 0:N], in0=zb[0:P, 2, 0:N], scalar=nr[:, t, D:D + 1], in1=later[:, t, :],
                                             op0=ALU.is_equal, op1=ALU.mult).then_inc(eq_done.sem, 1)
                for t in range(T):
                    dve.wait_ge(*eq_done.of(b, t + 1))
                    dve.scalar_tensor_tensor(out=less[:, t, 0:N], in0=zb[0:P, 2, 0:N], scalar=nr[:, t, D:D + 1], in1=eqm[:, t, 0:N],
                                             op0=ALU.is_gt, op1=ALU.add).then_inc(less_done.sem, 1)
                dve.wait_ge(*pl_ready.of(b))
                dve.tensor_scalar(pl_s[:], zb[0:C, 1, 2:3], 1e-6, None, ALU.add).then_inc(pl_steps.sem, 1)
                dve.wait_ge(*pl_steps.of(b, 1))
                dve.reciprocal(pl_r[:], pl_s[:]).then_inc(pl_steps.sem, 1)
                dve.wait_ge(*pl_steps.of(b, 2))
                dve.tensor_scalar(pl[:], zb[0:C, 1, 0:CT], pl_r[:], None, ALU.mult).then_inc(pl_steps.sem, 1)
                dve.wait_ge(*rk_ready.of(b))
                if not first(b):
                    dve.wait_ge(*mix_ready.before(b))
                dve.tensor_scalar(putT[:, 0:N], zb[0:Q, 3, 0:N], slot[:], None, ALU.is_equal).then_inc(putT_done.sem, 1)

            def queries(b):
                dve.wait_ge(*q_ready.of(b))
                if not first(b):
                    dve.wait_ge(*ql_ready.before(b))
                for c in range(CT):
                    ins = dve.tensor_tensor(qb[:, c, :, :], zb[0:C, 3, Q * c:Q * c + Q].unsqueeze(1).to_broadcast([C, H1 // 2, Q]),
                                            q_mask[:].unsqueeze(2).to_broadcast([C, H1 // 2, Q]), ALU.mult)
                ins.then_inc(qb_done.sem, 1)

            def attention_max(b):
                for j in range(IT):
                    dve.wait_ge(*ql_ready.of(b, j + 1))
                    if j == 0 and not first(b):
                        dve.wait_ge(*prob_done.before(b))
                    dve.tensor_reduce(nmax[:, j:j + 1], zb[:, j % 2, 0:N], AX.X, ALU.max, negate=True).then_inc(qmax_done.sem, 1)

            def attention_out(b):
                dve.wait_ge(*prob_done.of(b))
                dve.reciprocal(rsum_p[:], psum_p[:]).then_inc(rsum_done.sem, 1)
                dve.wait_ge(*rsum_done.of(b))
                dve.wait_ge(*pv_ready.of(b))
                if not first(b):
                    dve.wait_ge(*cxT_ready.before(b))
                cv = cx[:].rearrange("q (j a d) -> q j a d", j=IT, a=2)
                pv = zb[:, 0, 0:IT * 32].rearrange("q (j a d) -> q j a d", j=IT, a=2)
                dve.tensor_tensor(cv[:, :, 0, :], pv[0:Q, :, 0, :], rsum_p[0:Q, :].unsqueeze(2).to_broadcast([Q, IT, 16]), ALU.mult)
                dve.tensor_tensor(cv[:, :, 1, :], pv[Q:2 * Q, :, 1, :],
                                  rsum_p[Q:2 * Q, :].unsqueeze(2).to_broadcast([Q, IT, 16]), ALU.mult).then_inc(cx_done.sem, 1)
                dve.wait_ge(*ao_ready.of(b))
                dve.wait_ge(*ms_done.of(b))
                if not first(b):
                    dve.wait_ge(*mix_ready.before(b))
                dve.tensor_tensor(att[:], zb[0:Q, 1, 0:D], msel[:], ALU.subtract).then_inc(att_done.sem, 1)

            def fifth_norm(b):
                if not first(b):
                    dve.wait_ge(*h12_done.before(b))
                for k, (t0, t1) in enumerate(((0, 2), (2, 3))):
                    dve.wait_ge(*mix_ready.of(b, k + 1))
                    dve.tensor_tensor(h2[:, t0:t1, :], zb[0:P, 2 + k, 0:D * (t1 - t0)].rearrange("p (t d) -> p t d", d=D),
                                      zed[:, t0:t1, :], ALU.add).then_inc(h2_done.sem, 1)
                dve.wait_ge(*h2_done.of(b))
                norm(b, lambda t: h2[:, t, :], ln5, bn5, ag5)
                dve.wait_ge(*ag5.of(b))
                if not first(b):
                    dve.wait_ge(*n2T_ready.before(b))
                for t in range(T):
                    dve.scalar_tensor_tensor(out=n2[:, t, :], in0=h2[:, t, :], scalar=ln5[1][:, t, 0:1], in1=rows[:, 5, :],
                                             op0=ALU.subtract, op1=ALU.mult).then_inc(n2t_done.sem, 1)
                dve.wait_ge(*rs5.of(b))
                for t in range(T):
                    dve.wait_ge(*n2t_done.of(b, t + 1))
                    dve.scalar_tensor_tensor(out=n2[:, t, :], in0=n2[:, t, :], scalar=ln5[3][:, t:t + 1], in1=rows[:, 6, :],
                                             op0=ALU.mult, op1=ALU.add).then_inc(n2_done.sem, 1)

            def mix(b):
                depthwise(b)
                pool_pairs(b)
                spectrum_norm(b)
                second_norm(b)
                if first(b):
                    dve.wait_ge(rest_in.sem, REST)
                    dve.tensor_copy(head_sel[:], head_sel32).then_inc(consts.sem, 1)
                token_norms(b)
                token_softmax(b)
                token_products(b)
                third_norm(b)
                route(b)
                queries(b)
                attention_max(b)
                attention_out(b)
                fifth_norm(b)

            batches(dve, mix)

            def feed_forward(b, k, first_pair=False):
                if not first_pair:
                    dve.wait_ge(stored.sem, b * 16 - 16)
                for i, (t0, t1) in enumerate(((0, 2), (2, 3))):
                    dve.wait_ge(*w2_ready.of(b, i + 1))
                    dve.tensor_tensor(y_out[:, k, t0:t1, :], yb[0:P, i, 0:D * (t1 - t0)].rearrange("p (t d) -> p t d", d=D),
                                      hid[:, b, t0:t1, :], ALU.add).then_inc(y_done.sem, 1)

            dve.wait_ge(*h12_done.of(B - 1))
            for b in range(2):
                feed_forward(b, b, True)
            with dve.Fori(1, B // 2) as pair:
                feed_forward(2 * pair, 0)
                feed_forward(2 * pair + 1, 1)

        @block.gpsimd
        def _(pool):
            pool.memset(eps3[:], EPS).then_inc(consts.sem, 1)
            pool.memset(half3[:], -0.5).then_inc(consts.sem, 1)
            pool.wait_ge(consts.sem, 6)

            def rstd(b, buffers, ag, ve, rs):
                pool.wait_ge(*ag.of(b))
                pool.tensor_tensor(buffers[2][:], buffers[1][:, :, 1], eps3[:], ALU.add).then_inc(ve.sem, 1)
                pool.wait_ge(*ve.of(b))
                pool.tensor_tensor(buffers[3][:], buffers[2][:], half3[:], ALU.pow).then_inc(rs.sem, 1)

            def mix(b):
                if first(b):
                    pool.wait_ge(fft_in.sem, FFT)
                rstd(b, ln1, ag1, ve1, rs1)
                rstd(b, ln2, ag2, ve2, rs2)
                pool.wait_ge(*xh_done.of(b))
                pool.tensor_tensor(gate_p[:], eps3[0:1, 0:1], eps3[0:1, 0:1], ALU.add)
                pool.tensor_tensor(hid[:, b, :, :], hid[:, b, :, :], rows[:, 2:3, :].to_broadcast([P, T, D]), ALU.add)\
                    .then_inc(hb_done.sem, 1)
                pool.wait_ge(*ag3.of(b))
                var = ln3[1][:, :, 1]
                for i, (o, a, c, op) in enumerate(((ln3[2], var, eps3[:], ALU.add), (r3, ln3[2][:], half3[:], ALU.pow),
                                                   (r4a, r3[:], r3[:], ALU.mult), (r4b, r4a[:], var, ALU.mult),
                                                   (r4c, r4b[:], eps3[:], ALU.add), (r4b, r4c[:], half3[:], ALU.pow),
                                                   (r4, r4b[:], r3[:], ALU.mult))):
                    if i:
                        pool.wait_ge(*r_steps.of(b, i))
                    pool.tensor_tensor(o[:], a, c, op).then_inc(r_steps.sem, 1)
                pool.wait_ge(*nrt_done.of(b))
                pool.tensor_tensor(gate_p[:], eps3[0:1, 0:1], eps3[0:1, 0:1], ALU.add)
                pool.tensor_tensor(hid[:, b, :, :], hid[:, b, :, :], rows[:, 7:8, :].to_broadcast([P, T, D]), ALU.add)\
                    .then_inc(hz_done.sem, 1)
                pool.wait_ge(*h2_done.of(b))
                pool.wait_ge(*hz_done.of(b))
                pool.tensor_tensor(gate_p[:], eps3[0:1, 0:1], eps3[0:1, 0:1], ALU.add)
                pool.tensor_tensor(hid[:, b, :, :], hid[:, b, :, :], h2[:], ALU.add).then_inc(h12_done.sem, 1)
                rstd(b, ln5, ag5, ve5, rs5)

            batches(pool, mix)

        @block.scalar
        def _(act):
            for dst, name in rests:
                act.dma_start(dst if isinstance(dst, bass.AP) else dst[:], dram[name]).then_inc(rest_in.sem, 16)

            def mix(b):
                for t in range(T):
                    act.wait_ge(*pw_ready.of(b, t + 1))
                    if t == 0 and not first(b):
                        act.wait_ge(*pool_done.before(b))
                    act.activation(even[:, t, :], xb[0:P, t % 2, 0:D], ACT.Relu).then_inc(relu_done.sem, 1)
                act.wait_ge(*fa_ready.of(b))
                if not first(b):
                    act.wait_ge(*y_ready.before(b))
                act.activation(fc[:, :, 0:KF], xb[0:C, :, 0:KF], ACT.Copy)
                act.activation(fs[:, :, 0:KF], xb[0:C, :, KF:2 * KF], ACT.Copy)
                act.activation(fc[:, :, KF:N], xb[0:C, :, KF - 1:0:-1], ACT.Copy)
                act.activation(fs[:, :, KF:N], xb[0:C, :, 2 * KF - 1:KF:-1], ACT.Copy, scale=-1.0).then_inc(fcs_done.sem, 1)
                act.wait_ge(*xhT_ready.of(b))
                if not first(b):
                    act.wait_ge(*qkv_ready.before(b))
                act.activation(xhT[:, :, 0:N], xb[0:C, :, 0:N], ACT.Copy).then_inc(xhT_done.sem, 1)
                if first(b):
                    act.wait_ge(rest_in.sem, REST)
                    act.wait_ge(consts.sem, 6)
                for j in range(IT):
                    act.wait_ge(*qkv_ready.of(b, j + 1))
                    if j == 0 and not first(b):
                        act.wait_ge(*dots_done.before(b))
                        act.wait_ge(*o_ready.before(b))
                    act.activation(w_s[:, j, 0:N], yb[:, j % 2, 0:N], ACT.Copy)
                    act.activation(w_sq[:, j, 0:N], yb[:, j % 2, 0:N], ACT.Square, accum_out=nrm[:, j:j + 1]).then_inc(sq_done.sem, 1)
                act.wait_ge(*lmax_done.of(b))
                act.activation(lg[:, 0:N], lg[:, 0:N], ACT.Exp, bias=lgm[:, 0:1], accum_out=lgm[:, 1:2]).then_inc(lexp_done.sem, 1)
                act.wait_ge(*pi_steps.of(b, 7))
                act.activation(pi_mid[:], pi_r[:], ACT.Copy).then_inc(pi_mid0.sem, 1)
                act.wait_ge(*pi_mid0.of(b))
                act.activation(pi_parts[32:32 + H1, :], pi_mid[:], ACT.Copy).then_inc(pi_mid_sig.sem, 1)
                act.wait_ge(*nT_ready.of(b))
                if not first(b):
                    act.wait_ge(*mix_ready.before(b))
                act.activation(nT[0:C, :, 0:N], zb[0:C, 0:2, 0:N], ACT.Copy).then_inc(nT_done.sem, 1)
                act.wait_ge(*k_ready.of(b))
                if not first(b):
                    act.wait_ge(*ql_ready.before(b))
                for c in range(CT):
                    ins = act.activation(kT[:, c, 0:N], zb[0:C, 2 + c, 0:N], ACT.Identity, bias=b_k[:, c:c + 1])
                ins.then_inc(kT_done.sem, 1)
                for k, (t0, t1) in enumerate(((0, 2), (2, 3))):
                    src = zb[0:P, k, 0:(D + 1) * (t1 - t0)].rearrange("p (t d) -> p t d", d=D + 1)
                    act.wait_ge(*v_ready.of(b, k + 1))
                    if k == 0 and not first(b):
                        act.wait_ge(*pv_ready.before(b))
                    act.activation(sexp[:, t0:t1], src[:, :, D], ACT.Exp, scale=-1.0).then_inc(sexp_done.sem, 1)
                    act.activation(v[:, t0:t1, :], src[:, :, 0:D], ACT.Copy).then_inc(v_done.sem, 1)
                act.wait_ge(*less_done.of(b))
                act.activation(nT[C:C + 1, 1, 0:N], zb[C:C + 1, 2, 0:N], ACT.Copy).then_inc(sc_row_done.sem, 1)
                act.wait_ge(*pwm_ready.of(b))
                act.activation(w_m[C:C + 1, 1, :], zb[0:1, 1, 64:64 + D], ACT.Copy).then_inc(pwm_done.sem, 1)
                act.wait_ge(*put_ready.of(b))
                act.activation(put[:], zb[0:P, 0, 0:T * Q].rearrange("p (t q) -> p t q", q=Q), ACT.Copy).then_inc(put_done.sem, 1)
                act.wait_ge(*ns_ready.of(b))
                act.activation(nsT[0:C, 0, :], zb[0:C, 2, 0:Q], ACT.Copy)
                act.activation(nsT[:, 1, :], zb[0:C + 1, 2, Q:2 * Q], ACT.Copy).then_inc(ns_done.sem, 1)
                act.wait_ge(*ms_ready.of(b))
                if not first(b):
                    act.wait_ge(*att_done.before(b))
                act.activation(msel[:], zb[0:Q, 1, 0:D], ACT.Copy).then_inc(ms_done.sem, 1)

                def exponentials(j):
                    act.wait_ge(*qmax_done.of(b, j + 1))
                    if j == 0 and not first(b):
                        act.wait_ge(*prT_ready.before(b))
                        act.wait_ge(*rsum_done.before(b))
                    act.activation(probs[:, j, 0:N], zb[:, j % 2, 0:N], ACT.Exp, bias=nmax[:, j:j + 1],
                                   accum_out=psum_p[:, j:j + 1]).then_inc(prob_done.sem, 1)

                def transposed(j):
                    act.wait_ge(*prT_ready.of(b, j + 1))
                    act.activation(probsT[:, j, :, :], zb[0:P, 2 + j % 2, 0:T * 128].rearrange("p (t q) -> p t q", q=128),
                                   ACT.Copy).then_inc(prT_done.sem, 1)

                for j in range(IT):
                    exponentials(j)
                    if j:
                        transposed(j - 1)
                transposed(IT - 1)
                act.wait_ge(*cxT_ready.of(b))
                act.activation(cxT[0:C, :, :], zb[0:C, 0, 0:2 * Q].rearrange("p (c q) -> p c q", q=Q), ACT.Copy).then_inc(cxT_done.sem, 1)
                act.wait_ge(*n2T_ready.of(b))
                act.activation(n2T[:, b, :, 0:N], zb[0:C, 0:2, 0:N], ACT.Copy).then_inc(n2T_done.sem, 1)

            batches(act, mix)

            def feed_forward(b, k, first_pair=False):
                for j in range(IT):
                    act.wait_ge(*w1_ready.of(b, j + 1))
                    if j == 0 and not first_pair:
                        act.wait_ge(w2_ready.sem, b * 2 - 2)
                    act.activation(gelu[k][:, j, 0:N], xb[:, j % 2, 0:N], ACT.Gelu, bias=b_1[:, j:j + 1]).then_inc(gelu_done.sem, 1)

            for b in range(2):
                feed_forward(b, b, True)
            with act.Fori(1, B // 2) as pair:
                feed_forward(2 * pair, 0)
                feed_forward(2 * pair + 1, 1)

        @block.tensor
        def _(pe):
            mm = pe.matmul

            def transposes(b, src, dst):
                for c in range(CT):
                    for t in range(T):
                        ins = pe.transpose(dst[0:C, c, tok(t)], src[:, t, chan(c)], ident[0:P, 0:P])
                return ins

            pe.wait_ge(first_in.sem, FIRST)

            def mix(b):
                pe.wait_ge(*dw_done.of(b))
                for t in range(T):
                    if t == 2:
                        pe.wait_ge(*pool_done.of(b, 1))
                    elif not first(b):
                        pe.wait_ge(*xhT_done.before(b))
                    for e in range(2):
                        f0 = 2 * P * t + e
                        o = xb[0:P, t % 2, D * e:D * e + D]
                        mm(o, dw[0:C + 1, 0, f0:f0 + 2 * P - 1:2], w_pw[:, 0, :], start=True, stop=False)
                        ins = mm(o, dw[0:C, 1, f0:f0 + 2 * P - 1:2], w_pw[0:C, 1, :], start=False, stop=True)
                    ins.then_inc(pw_ready.sem, 1)
                if first(b):
                    pe.wait_ge(fft_in.sem, FFT)
                pe.wait_ge(*pool_done.of(b))
                for c in range(CT):
                    for t in range(T):
                        ins = mm(xb[0:C, c, 0:2 * KF], pooled_h[:, t, chan(c)], dft_n[:, t, :], start=(t == 0), stop=(t == T - 1))
                ins.then_inc(fa_ready.sem, 1)
                pe.wait_ge(*fcs_done.of(b))
                for t in range(T):
                    o = xb[0:P, t // 2, D * (t % 2):D * (t % 2) + D]
                    for i, (f, r) in enumerate(((fc, 0), (fs, 1))):
                        for c in range(CT):
                            ins = mm(o, f[:, c, tok(t)], dft_d[:, r, c, :], start=(i + c == 0), stop=(i + c == 2))
                    if t:
                        ins.then_inc(y_ready.sem, 1)
                pe.wait_ge(*xh_done.of(b))
                transposes(b, xh, xb).then_inc(xhT_ready.sem, 1)
                pe.wait_ge(*xhT_done.of(b))
                for j in range(IT):
                    if j >= 2:
                        pe.wait_ge(*sq_done.of(b, j - 1))
                    elif not first(b):
                        pe.wait_ge(*h1_done.before(b))
                    for c in range(CT):
                        ins = mm(yb[:, j % 2, 0:N], w_qkv[:, c, 128 * j:128 * j + 128], xhT[:, c, 0:N], start=(c == 0), stop=(c == 1))
                    ins.then_inc(qkv_ready.sem, 1)
                pe.wait_ge(*rhead_done.of(b))
                for j in range(IT):
                    ins = mm(yb[0:H1, 0, 0:N], rhead[:, j, :], w_sq[:, j, 0:N], start=(j == 0), stop=(j == IT - 1))
                ins.then_inc(lg_ready.sem, 1)
                if first(b):
                    pe.wait_ge(consts.sem, 7)
                pe.wait_ge(*pi_low_done.of(b))
                for j in range(IT):
                    if j >= 2:
                        pe.wait_ge(*u_done.of(b, j - 1))
                    ins = mm(yb[:, j % 2, 0:NE], head_sel[:, j, :], pi_parts[:], start=True, stop=True)
                    ins.then_inc(pib_ready.sem, 1)
                pe.wait_ge(*woa_done.of(b))
                for t in range(T):
                    o = yb[0:P, t // 2, D * (t % 2):D * (t % 2) + D]
                    for j in range(IT):
                        ins = mm(o, u[:, j, tok(t)], w_oa[:, j, :], start=(j == 0), stop=(j == IT - 1))
                    if t:
                        ins.then_inc(o_ready.sem, 1)
                pe.wait_ge(*nr_done.of(b))
                if not first(b):
                    pe.wait_ge(*n2T_done.before(b))
                transposes(b, nr, zb).then_inc(nT_ready.sem, 1)
                pe.wait_ge(*nT_done.of(b))
                if not first(b):
                    pe.wait_ge(*h2_done.before(b))
                for k in range(CT):
                    for c in range(CT):
                        ins = mm(zb[0:C, 2 + k, 0:N], w_k[:, c, chan(k)], nT[0:C, c, 0:N], start=(c == 0), stop=(c == 1))
                ins.then_inc(k_ready.sem, 1)
                for t in range(T):
                    o = zb[0:P, t // 2, (D + 1) * (t % 2):(D + 1) * (t % 2) + D + 1]
                    mm(o, nT[:, 0, tok(t)], w_v[:, 0, :], start=True, stop=False)
                    ins = mm(o, nT[0:C, 1, tok(t)], w_v[0:C, 1, :], start=False, stop=True)
                    if t:
                        ins.then_inc(v_ready.sem, 1)
                pe.wait_ge(*kT_done.of(b))
                pe.wait_ge(*sc_steps.of(b))
                for t in range(T):
                    ins = pe.transpose(zb[0:P, 2, tok(t)], nr[:, t, D:D + 1].to_broadcast([P, P]), ident[0:P, 0:P])
                ins.then_inc(sb_ready.sem, 1)
                pe.wait_ge(*v_done.of(b))
                for c in range(CT + 1):
                    for t in range(T):
                        lhs = ones[:] if c == CT else nr[:, t, chan(c)]
                        ins = mm(zb[0:C, 1, c:c + 1], lhs, nr[:, t, D:D + 1], start=(t == 0), stop=(t == T - 1))
                ins.then_inc(pl_ready.sem, 1)
                pe.wait_ge(*pl_steps.of(b))
                for c in range(CT):
                    ins = mm(zb[0:1, 1, 64:64 + D], pl[:, c:c + 1], w_m[0:C, c, :], start=(c == 0), stop=(c == 1))
                ins.then_inc(pwm_ready.sem, 1)
                pe.wait_ge(*less_done.of(b))
                for t in range(T):
                    ins = mm(zb[0:Q, 3, 0:N], ones_bf[:], less[:, t, 0:N], start=(t == 0), stop=(t == T - 1))
                ins.then_inc(rk_ready.sem, 1)
                pe.wait_ge(*putT_done.of(b))
                for t in range(T):
                    ins = mm(zb[0:P, 0, Q * t:Q * t + Q], putT[:, tok(t)], ident[0:Q, 0:Q], start=True, stop=True)
                ins.then_inc(put_ready.sem, 1)
                pe.wait_ge(*sc_row_done.of(b))
                pe.wait_ge(*put_done.of(b))
                for c in range(CT):
                    rows_of = chan(0) if c == 0 else slice(C, D + 1)
                    for t in range(T):
                        ins = mm(zb[0:C + c, 2, Q * c:Q * c + Q], nr[:, t, rows_of], put[:, t, :], start=(t == 0), stop=(t == T - 1))
                ins.then_inc(ns_ready.sem, 1)
                pe.wait_ge(*ns_done.of(b))
                for k in range(CT):
                    o = zb[0:C, 3, Q * k:Q * k + Q]
                    mm(o, w_q[:, 0, chan(k)], nsT[:, 0, :], start=True, stop=False)
                    ins = mm(o, w_q[0:C, 1, chan(k)], nsT[0:C, 1, :], start=False, stop=True)
                ins.then_inc(q_ready.sem, 1)
                pe.wait_ge(*pwm_done.of(b))
                for c in range(CT):
                    ins = mm(zb[0:Q, 1, 0:D], nsT[:, c, :], w_m[:, c, :], start=(c == 0), stop=(c == 1))
                ins.then_inc(ms_ready.sem, 1)

                def logits(j):
                    if j == 0:
                        pe.wait_ge(*qb_done.of(b))
                    if j == 1:
                        pe.wait_ge(*ms_done.of(b))
                    if j >= 2:
                        pe.wait_ge(*prob_done.of(b, j - 1))
                    c, i = divmod(j, 3)
                    mm(zb[:, j % 2, 0:N], qb[:, c, 2 * i:2 * i + 2, :].rearrange("p h q -> p (h q)"), kT[:, c, 0:N],
                       start=True, stop=True).then_inc(ql_ready.sem, 1)

                def turn(j):
                    if j >= 2:
                        pe.wait_ge(*prT_done.of(b, j - 1))
                    pe.wait_ge(*prob_done.of(b, j + 1))
                    for t in range(T):
                        ins = pe.transpose(zb[0:P, 2 + j % 2, 128 * t:128 * t + 128], probs[:, j, tok(t)], ident[:])
                    ins.then_inc(prT_ready.sem, 1)

                for j in range(IT):
                    logits(j)
                    if j:
                        turn(j - 1)
                turn(IT - 1)
                for j in range(IT):
                    pe.wait_ge(*prT_done.of(b, j + 1))
                    for t in range(T):
                        ins = mm(zb[:, 0, 32 * j:32 * j + 32], probsT[:, j, t, :], v[:, t, 32 * j:32 * j + 32],
                                 start=(t == 0), stop=(t == T - 1))
                ins.then_inc(pv_ready.sem, 1)
                pe.wait_ge(*cx_done.of(b))
                for c in range(CT):
                    ins = mm(zb[0:C, 0, Q * c:Q * c + Q], cx[:, chan(c)], ident[0:Q, 0:Q], start=True, stop=True)
                ins.then_inc(cxT_ready.sem, 1)
                pe.wait_ge(*cxT_done.of(b))
                mm(zb[0:Q, 1, 0:D], cxT[:, 0, :], w_o[:, 0, :], start=True, stop=False)
                mm(zb[0:Q, 1, 0:D], cxT[0:C, 1, :], w_o[0:C, 1, :], start=False, stop=True).then_inc(ao_ready.sem, 1)
                pe.wait_ge(*att_done.of(b))
                for t in range(T):
                    o = zb[0:P, 2 + t // 2, D * (t % 2):D * (t % 2) + D]
                    for c in range(CT):
                        mm(o, nT[:, c, tok(t)], w_m[:, c, :], start=(c == 0), stop=False)
                    ins = mm(o, putT[:, tok(t)], att[:], start=False, stop=True)
                    if t:
                        ins.then_inc(mix_ready.sem, 1)
                pe.wait_ge(*n2_done.of(b))
                transposes(b, n2, zb).then_inc(n2T_ready.sem, 1)

            batches(pe, mix)

            def feed_forward(b, k, first_pair=False):
                for j in range(IT):
                    if j >= 2:
                        pe.wait_ge(*gelu_done.of(b, j - 1))
                    elif not (first_pair and k == 0):
                        pe.wait_ge(*gelu_done.before(b, IT - 1 + j))
                    for c in range(CT):
                        ins = mm(xb[:, j % 2, 0:N], w_1[:, c, 128 * j:128 * j + 128], n2T[:, b, c, 0:N], start=(c == 0), stop=(c == 1))
                    ins.then_inc(w1_ready.sem, 1)
                if not (first_pair and k == 0):
                    pe.wait_ge(*y_done.before(b))
                pe.wait_ge(*gelu_done.of(b))
                for t in range(T):
                    o = yb[0:P, t // 2, D * (t % 2):D * (t % 2) + D]
                    for j in range(IT):
                        ins = mm(o, gelu[k][:, j, tok(t)], w_2[:, j, :], start=(j == 0), stop=(j == IT - 1))
                    if t:
                        ins.then_inc(w2_ready.sem, 1)

            pe.wait_ge(*n2T_done.of(B - 1))
            for b in range(2):
                feed_forward(b, b, True)
            with pe.Fori(1, B // 2) as pair:
                feed_forward(2 * pair, 0)
                feed_forward(2 * pair + 1, 1)


def kernel(**inputs):
    import numpy as np
    import concourse.bacc as bacc
    from concourse.bass_utils import run_bass_kernel_spmd as run

    f = np.float32
    a = {k: np.asarray(v) for k, v in inputs.items()}

    def tiles(w, p):
        return np.ascontiguousarray(w.reshape(-1, p, w.shape[-1]).transpose(1, 0, 2))

    def with_row(w, row):
        extra = np.stack([row, np.zeros_like(row)])[None]
        return np.concatenate([tiles(w, C), extra], 0)

    x = np.zeros((B, CT, C, S + 6), f)
    x[:, :, :, 3:3 + S] = a["x"].transpose(0, 2, 1).reshape(B, CT, C, S)
    n, k, d = np.arange(N), np.arange(KF), np.arange(D)
    turn_n = 2 * np.pi * ((n[:, None] * k) % N) / N
    turn_d = 2 * np.pi * ((d[:, None] * d) % D) / D
    p128, q = np.arange(128), np.arange(Q)
    head = 2 * np.arange(IT)[None, :] + (p128 // 64)[:, None]
    sel = np.zeros((96, IT, 128), f)
    for r in (0, 32, 64):
        sel[r:r + H1] = (head.T[None] == np.arange(H1)[:, None, None])
    m = (P * np.arange(T)[None, :] + np.arange(P)[:, None])[:, :, None]
    data = {
        "x": np.ascontiguousarray(x.transpose(0, 2, 1, 3)),
        "w_dw": tiles(np.concatenate([a["L0_tok_w_dw"][:, 0], a["L0_tok_b_dw"][:, None]], 1), C),
        "w_pw": with_row(a["L0_tok_w_pw"][:, :, 0].T, a["L0_tok_b_pw"]),
        "ones_row": np.ones((1, S), f),
        "dft_n": tiles(np.concatenate([np.cos(turn_n), np.sin(turn_n)], 1), P).astype(f),
        "dft_d": np.stack([tiles(np.cos(turn_d), C), tiles(-np.sin(turn_d), C)], 1).astype(f),
        "rows": np.broadcast_to(np.stack([a["L0_tok_gamma"], a["L0_tok_beta"], a["L0_attn_b_out"], a["L0_ffn_g1"], a["L0_ffn_b1"],
                                          a["L0_ffn_g2"], a["L0_ffn_b2"], a["L0_ffn_bf2"]]), (P, 8, D)),
        "ident": np.eye(128, dtype=f),
        "w_qkv": tiles(a["L0_attn_w_qkv"], C),
        "temp": a["L0_attn_temp"],
        "head_mask": (head[:, :, None] == np.arange(H1)).astype(f),
        "head_sel": sel,
        "w_out": tiles(a["L0_attn_w_out"], 128),
        "w_k": tiles(a["L0_ffn_Wk"], C),
        "b_k": a["L0_ffn_bk"].reshape(CT, C).T,
        "w_v": with_row(np.concatenate([a["L0_ffn_Wv"], a["L0_ffn_Wr"][:, None]], 1),
                        np.concatenate([a["L0_ffn_bv"], a["L0_ffn_br"].reshape(1)])),
        "w_q": with_row(a["L0_ffn_Wq"], a["L0_ffn_bq"]),
        "w_o": with_row(a["L0_ffn_Wo"], a["L0_ffn_bo"]),
        "w_m": with_row(a["L0_ffn_Wm"], a["L0_ffn_bm"]),
        "q_mask": 0.25 * (np.arange(C)[:, None] // 16 == np.arange(H1 // 2)).astype(f),
        "later": (n[None, None, :] > m).astype(f),
        "slot": np.where(q < SEL, q, -1).astype(f)[:, None],
        "w_1": tiles(a["L0_ffn_W1"], C),
        "b_1": a["L0_ffn_bf1"].reshape(IT, 128).T,
        "w_2": tiles(a["L0_ffn_W2"], 128),
        "ones_n": np.ones((1, N), f), "ones_q": np.ones((1, Q), f), "ones_q2": np.ones((1, Q), f),
    }
    nc = bacc.Bacc("TRN2", target_bir_lowering=False, num_devices=1)
    arrays, dram = {}, {}
    for name, value in data.items():
        value = np.ascontiguousarray(value)
        assert value.dtype == f, name
        arrays[f"in_{name}"] = value
        dram[name] = nc.dram_tensor(f"in_{name}", value.shape, mybir.dt.float32, kind="ExternalInput").ap()
    out = nc.dram_tensor("out_0", (B, N, D), mybir.dt.float32, kind="ExternalOutput").ap()
    audio_tower(nc, dram, out)
    result = run(nc, [arrays], core_ids=[0])
    return result.results[0]["out_0"]
```

```python
import concourse.bass as bass
from concourse import mybir
from contextlib import ExitStack

B, S, D, K = 8, 750, 192, 7
N = S // 2
P, T = 125, 3
C, CT = 96, 2
H1, IT = 12, 6
KF = N // 2 + 1
NE = N + 1
SEL = int(round(0.15 * N))
Q = 64
EPS = 1e-5


class Signal:

    def __init__(self, sem, per_batch):
        self.sem, self.per_batch = sem, per_batch

    def of(self, b, j=None):
        return self.sem, b * self.per_batch + (self.per_batch if j is None else j)

    def before(self, b, j=None):
        j = self.per_batch if j is None else j
        return self.sem, b * self.per_batch + (j - self.per_batch)


def audio_tower(nc, dram, out):
    fp32, bf16 = mybir.dt.float32, mybir.dt.bfloat16
    ALU, ACT, AX = mybir.AluOpType, mybir.ActivationFunctionType, mybir.AxisListType

    with ExitStack() as ctx:
        def sb(name, shape, dt=fp32):
            return ctx.enter_context(nc.sbuf_tensor(name, shape, dt))

        def signal(name, per_batch=1):
            return Signal(ctx.enter_context(nc.semaphore(name)), per_batch)

        x_in = sb("x_in", [C, CT, S + 6])
        w_dw = sb("w_dw_sb", [C, CT, K + 1])
        w_pw = sb("w_pw_sb", [C + 1, CT, D])
        dft_n = sb("dft_n_sb", [P, T, 2 * KF])
        dft_d = sb("dft_d_sb", [C, 2, CT, D])
        ident = sb("ident_sb", [128, 128])
        rows = sb("rows_sb", [P, 8, D])
        w_qkv = sb("w_qkv_sb", [C, CT, IT * 128])
        temp = sb("temp_sb", [H1, 1])
        head_mask = sb("head_mask_sb", [128, IT, H1])
        head_sel = sb("head_sel_sb", [96, IT, 128], bf16)
        w_out = sb("w_out_sb", [128, IT, D])
        w_k = sb("w_k_sb", [C, CT, D])
        b_k = sb("b_k_sb", [C, CT])
        w_v = sb("w_v_sb", [C + 1, CT, D + 1])
        w_q = sb("w_q_sb", [C + 1, CT, D])
        w_o = sb("w_o_sb", [C + 1, CT, D])
        w_m = sb("w_m_sb", [C + 1, CT, D])
        q_mask = sb("q_mask_sb", [C, H1 // 2])
        later = sb("later_sb", [P, T, N])
        slot = sb("slot_sb", [Q, 1])
        w_1 = sb("w_1_sb", [C, CT, IT * 128])
        b_1 = sb("b_1_sb", [128, IT])
        w_2 = sb("w_2_sb", [128, IT, D])
        eps3 = sb("eps3", [P, T])
        half3 = sb("half3", [P, T])
        ones = sb("ones", [P, C])
        gate_p = sb("gate_p", [1, 1])
        ones_bf = sb("ones_bf", [P, Q], bf16)

        res = sb("res", [P, T, D])
        res_q = sb("res_q", [P, T, D])
        zed = sb("zed", [P, T, D])
        n2T = sb("n2T", [C, CT, NE])

        dw = sb("dw", [C + 1, CT, S])
        even = sb("even", [P, T, D])
        pooled_h = sb("pooled_h", [P, T, D])
        fc = sb("fc", [C, CT, NE])
        fs = sb("fs", [C, CT, NE])
        xh = sb("xh", [P, T, D])
        xhT = sb("xhT", [C, CT, NE])

        def norm_buffers(n):
            return (sb(f"st{n}", [P, T, 6]), sb(f"ag{n}", [P, T, 2]), sb(f"ve{n}", [P, T]), sb(f"rs{n}", [P, T]),
                    sb(f"gate{n}", [1, 1]))

        ln1, ln2, ln3, ln5 = (norm_buffers(n) for n in (1, 2, 3, 5))

        w_s = sb("w_s", [128, IT, NE])
        w_sq = sb("w_sq", [128, IT, NE])
        nrm = sb("nrm", [128, IT])
        rnrm = sb("rnrm", [128, IT])
        rhead = sb("rhead", [128, IT, H1])
        lg = sb("lg", [H1, NE])
        lgm = sb("lgm", [H1, 4])
        pi = sb("pi", [H1, NE])
        pi_r = sb("pi_r", [H1, NE])
        pi_mid = sb("pi_mid", [H1, NE], bf16)
        pi_parts = sb("pi_parts", [96, NE], bf16)
        u = w_sq
        junk = sb("junk", [128, 2, NE])
        dots = sb("dots", [128, IT])
        natt = sb("natt", [128, IT])
        w_oa = sb("w_oa", [128, IT, D])
        r3 = sb("r3", [P, T])
        r4a = sb("r4a", [P, T])
        r4b = sb("r4b", [P, T])
        r4c = sb("r4c", [P, T])
        r4 = sb("r4", [P, T])

        nr = sb("nr", [P, T, D + 1])
        nT = sb("nT", [C + 1, CT, NE])
        kT = sb("kT", [C, CT, NE])
        v = sb("v", [P, T, D])
        sexp = sb("sexp", [P, T])
        eqm = sb("eqm", [P, T, NE], bf16)
        less = eqm
        putT = sb("putT", [Q, NE])
        put = sb("put", [P, T, Q])
        pl_s = sb("pl_s", [C, 1])
        pl_r = sb("pl_r", [C, 1])
        pl = sb("pl", [C, CT])
        nsT = sb("nsT", [C + 1, CT, Q])
        msel = sb("msel", [Q, D])
        qb = sb("qb", [C, CT, H1 // 2, Q])
        nmax = sb("nmax", [128, IT])
        psum_p = sb("psum_p", [128, IT])
        rsum_p = sb("rsum_p", [128, IT])
        probs = sb("probs", [128, IT, NE])
        head_sel32 = probs[0:96, :, 0:128]
        probsT = sb("probsT", [P, IT, T, 128])
        cx = sb("cx", [Q, D])
        cxT = sb("cxT", [C + 1, CT, Q])
        att = sb("att", [Q, D])
        n2 = sb("n2", [P, T, D])
        h2 = sb("h2", [P, T, D])

        gelu = probs
        y_out = sb("y_out", [P, T, D])

        xb = ctx.enter_context(nc.psum_tensor("xb", [128, 2, 512], fp32))
        yb = ctx.enter_context(nc.psum_tensor("yb", [128, 2, 512], fp32))
        zb = ctx.enter_context(nc.psum_tensor("zb", [128, 4, 512], fp32))

        first_in = signal("first_in", 16)
        x_ready = signal("x_ready", 16)
        fft_in = signal("fft_in", 16)
        rest_in = signal("rest_in", 16)
        consts = signal("consts")
        dw_done = signal("dw_done", CT * (K))
        pw_ready, relu_done, pool_done = signal("pw_ready", T), signal("relu_done", T), signal("pool_done", T)
        fa_ready, fcs_done = signal("fa_ready"), signal("fcs_done")
        y_ready = signal("y_ready", 2)
        bn1, ag1, ve1, rs1 = signal("bn1"), signal("ag1"), signal("ve1"), signal("rs1")
        lnt_done, h0_done = signal("lnt_done", T), signal("h0_done", T)
        bn2, ag2, ve2, rs2 = signal("bn2"), signal("ag2"), signal("ve2"), signal("rs2")
        xh_done, xhT_ready, xhT_done = signal("xh_done", T), signal("xhT_ready"), signal("xhT_done")
        qkv_ready, sq_done = signal("qkv_ready", IT), signal("sq_done", IT)
        rn1, rn2, rhead_done = signal("rn1"), signal("rn2"), signal("rhead_done")
        lg_ready, lg_done, lmax_done, lexp_done = signal("lg_ready"), signal("lg_done"), signal("lmax_done"), signal("lexp_done")
        pi_steps, pi_mid0, pi_mid_sig, pi_low_done = signal("pi_steps", 7), signal("pi_mid"), signal("pi_mid_done"), signal("pi_low_done")
        pib_ready, u_done, dots_done = signal("pib_ready", IT), signal("u_done", IT), signal("dots_done", IT)
        att_steps, woa_done = signal("att_steps", 3), signal("woa_done")
        o_ready = signal("o_ready", 2)
        hb_done, h1_done = signal("hb_done"), signal("h1_done", 2)
        bn3, ag3, r_steps = signal("bn3"), signal("ag3"), signal("r_steps", 7)
        z_done, nrt_done, nr_done = signal("z_done", T), signal("nrt_done", T), signal("nr_done", T)
        nT_ready, nT_done, sc_row_done = signal("nT_ready"), signal("nT_done"), signal("sc_row_done")
        k_ready, kT_done = signal("k_ready"), signal("kT_done")
        v_ready, v_done, sexp_done = signal("v_ready", 2), signal("v_done", 2), signal("sexp_done", 2)
        sc_steps = signal("sc_steps", 2)
        sb_ready, less_done, eq_done = signal("sb_ready"), signal("less_done", T), signal("eq_done", T)
        rk_ready, putT_done = signal("rk_ready"), signal("putT_done")
        put_ready, put_done = signal("put_ready"), signal("put_done")
        pl_ready, pl_steps, pwm_ready, pwm_done = signal("pl_ready"), signal("pl_steps", 3), signal("pwm_ready"), signal("pwm_done")
        ns_ready, ns_done = signal("ns_ready"), signal("ns_done")
        q_ready, qb_done = signal("q_ready"), signal("qb_done")
        ms_ready, ms_done = signal("ms_ready"), signal("ms_done")
        ql_ready, qmax_done, prob_done = signal("ql_ready", IT), signal("qmax_done", IT), signal("prob_done", IT)
        prT_ready, prT_done = signal("prT_ready", IT), signal("prT_done", IT)
        pv_ready, rsum_done, cx_done = signal("pv_ready"), signal("rsum_done"), signal("cx_done")
        cxT_ready, cxT_done = signal("cxT_ready"), signal("cxT_done")
        ao_ready, att_done = signal("ao_ready"), signal("att_done")
        mix_ready, h2_done = signal("mix_ready", 2), signal("h2_done", 2)
        hz_done, h12_done = signal("hz_done"), signal("h12_done")
        bn5, ag5, ve5, rs5 = signal("bn5"), signal("ag5"), signal("ve5"), signal("rs5")
        n2t_done, n2_done = signal("n2t_done", T), signal("n2_done", T)
        n2T_ready, n2T_done = signal("n2T_ready"), signal("n2T_done")
        w1_ready, gelu_done = signal("w1_ready", IT), signal("gelu_done", IT)
        w2_ready, y_done, stored = signal("w2_ready", 2), signal("y_done", 2), signal("stored", 16)

        block = ctx.enter_context(nc.Block())

        def tok(t):
            return slice(P * t, P * (t + 1))

        def chan(c):
            return slice(C * c, C * (c + 1))

        firsts = [(w_dw, "w_dw"), (w_pw, "w_pw"), (dw[C:C + 1, 0, :], "ones_row")]
        ffts = [(dft_n, "dft_n"), (dft_d, "dft_d"), (rows, "rows"), (ident, "ident"), (w_qkv, "w_qkv")]
        rests = [(temp, "temp"), (head_mask, "head_mask"), (head_sel32, "head_sel"), (w_out, "w_out"), (w_k, "w_k"),
                 (b_k, "b_k"), (w_v, "w_v"), (w_q, "w_q"), (w_o, "w_o"), (w_m, "w_m"), (q_mask, "q_mask"),
                 (later, "later"), (slot, "slot"), (w_1, "w_1"), (b_1, "b_1"), (w_2, "w_2"),
                 (nT[C:C + 1, 0, 0:N], "ones_n"), (nsT[C:C + 1, 0, :], "ones_q"), (cxT[C:C + 1, 0, :], "ones_q2")]
        FIRST, FFT, REST = (16 * len(x) for x in (firsts, ffts, rests))

        def pipeline(eng, step):
            step(0, None, 1)
            step(1, 0, 2)
            with eng.Fori(2, B - 1) as i:
                step(i, i - 1, i + 1)
            step(B - 1, B - 2, None)
            step(None, B - 1, None)

        def first(b):
            return isinstance(b, int) and b == 0

        @block.sync
        def _(sp):
            for dst, name in firsts:
                sp.dma_start(dst if isinstance(dst, bass.AP) else dst[:], dram[name]).then_inc(first_in.sem, 16)
            sp.dma_start(x_in[:], dram["x"][0]).then_inc(x_ready.sem, 16)
            for dst, name in ffts:
                sp.dma_start(dst[:], dram[name]).then_inc(fft_in.sem, 16)

            def load(b):
                sp.wait_ge(*dw_done.before(b))
                sp.dma_start(x_in[:], dram["x"][b]).then_inc(x_ready.sem, 16)

            def store(b):
                done, ring = y_done.of(b)[1], stored.before(b)[1]
                if not first(b):
                    done, ring = (v if isinstance(v, int) else sp.snap(v) for v in (done, ring))
                    sp.wait_ge(stored.sem, ring)
                sp.wait_ge(y_done.sem, done)
                sp.wait_ge(first_in.sem, FIRST)
                sp.dma_start(out[b].rearrange("(t p) d -> p t d", p=P), y_out[:]).then_inc(stored.sem, 16)

            load(1)
            load(2)
            load(3)
            store(0)
            with sp.Fori(2, B - 2) as i:
                load(i + 2)
                store(i - 1)
            for b in range(B - 3, B):
                store(b)
            sp.wait_ge(*stored.of(B - 1))

        @block.vector
        def _(dve):
            dve.memset(ones[:], 1.0).then_inc(consts.sem, 1)
            dve.memset(ones_bf[:], 1.0).then_inc(consts.sem, 1)
            dve.memset(w_s[:, :, N:NE], 1.0).then_inc(consts.sem, 1)
            dve.memset(pi_parts[:], 0.0).then_inc(consts.sem, 1)
            dve.wait_ge(first_in.sem, FIRST)

            def stats(src, buffers, bn):
                for t in range(T):
                    ins = dve.bn_stats(buffers[0][:, t, :], src[:, t, :])
                ins.then_inc(bn.sem, 1)

            def aggregate(b, buffers, bn, ag):
                dve.wait_ge(*bn.of(b))
                dve.memset(buffers[4][:], 0.0)
                for t in range(T):
                    ins = dve.bn_aggr(buffers[1][:, t, :], buffers[0][:, t, :])
                ins.then_inc(ag.sem, 1)

            def depthwise(b, k0, k1):
                if b is None:
                    return
                if k0 == 0:
                    dve.wait_ge(*x_ready.of(b))
                    if not first(b):
                        dve.wait_ge(*pw_ready.before(b))
                for k in range(k0, k1):
                    for c in range(CT):
                        src = x_in[:, c, k:k + S]
                        if k == 0:
                            ins = dve.tensor_scalar(dw[0:C, c, :], src, w_dw[:, c, 0:1], w_dw[:, c, K:K + 1], ALU.mult, ALU.add)
                        else:
                            dve.wait_ge(*dw_done.of(b, CT * (k - 1) + c + 1))
                            ins = dve.scalar_tensor_tensor(out=dw[0:C, c, :], in0=src, scalar=w_dw[:, c, k:k + 1],
                                                           in1=dw[0:C, c, :], op0=ALU.mult, op1=ALU.add)
                        ins.then_inc(dw_done.sem, 1)

            def pool_pairs(b):
                if not first(b):
                    dve.wait_ge(*fa_ready.before(b))
                for t in range(T):
                    dve.wait_ge(*relu_done.of(b, t + 1))
                    src = (xb[0:P, 0], xb[0:P, 1], yb[0:P, 0])[t]
                    dve.scalar_tensor_tensor(out=pooled_h[:, t, :], in0=src[:, D:2 * D], scalar=0.0, in1=even[:, t, :],
                                             op0=ALU.max, op1=ALU.max).then_inc(pool_done.sem, 1)


            def spectrum(t):
                return xb[0:P, t // 2, D * (t % 2):D * (t % 2) + D]

            def spectrum_stats(b):
                for t in range(T):
                    if t in (0, 2):
                        dve.wait_ge(*y_ready.of(b, 1 + t // 2))
                    ins = dve.bn_stats(ln1[0][:, t, :], spectrum(t))
                ins.then_inc(bn1.sem, 1)
                aggregate(b, ln1, bn1, ag1)
                dve.wait_ge(*ag1.of(b))
                if first(b):
                    dve.wait_ge(fft_in.sem, FFT)
                else:
                    dve.wait_ge(*hz_done.before(b))
                for t in range(T):
                    dve.scalar_tensor_tensor(out=res[:, t, :], in0=spectrum(t), scalar=ln1[1][:, t, 0:1], in1=rows[:, 0, :],
                                             op0=ALU.subtract, op1=ALU.mult).then_inc(lnt_done.sem, 1)

            def spectrum_norm(b):
                dve.wait_ge(*rs1.of(b))
                dve.wait_ge(*lnt_done.of(b))
                for t in range(T):
                    dve.scalar_tensor_tensor(out=res[:, t, :], in0=res[:, t, :], scalar=ln1[3][:, t:t + 1], in1=rows[:, 1, :],
                                             op0=ALU.mult, op1=ALU.add).then_inc(h0_done.sem, 1)
                dve.wait_ge(*h0_done.of(b))
                stats(res, ln2, bn2)
                aggregate(b, ln2, bn2, ag2)

            def second_norm(b):
                dve.wait_ge(*ag2.of(b))
                dve.wait_ge(*rs2.of(b))
                if not first(b):
                    dve.wait_ge(*xhT_ready.before(b))
                for t in range(T):
                    dve.tensor_scalar(xh[:, t, :], res[:, t, :], ln2[1][:, t, 0:1], ln2[3][:, t:t + 1],
                                      ALU.subtract, ALU.mult).then_inc(xh_done.sem, 1)

            def token_norms(b):
                dve.wait_ge(*sq_done.of(b))
                dve.tensor_scalar(nrm[:], nrm[:], 1e-24, None, ALU.max).then_inc(rn1.sem, 1)
                dve.wait_ge(*rn1.of(b))
                dve.reciprocal(rnrm[:], nrm[:]).then_inc(rn2.sem, 1)
                dve.wait_ge(*rn2.of(b))
                dve.tensor_tensor(rhead[:], head_mask[:], rnrm[:].unsqueeze(2).to_broadcast([128, IT, H1]), ALU.mult)\
                   .then_inc(rhead_done.sem, 1)

            def token_max(b):
                dve.wait_ge(*lg_ready.of(b))
                dve.tensor_scalar(lg[:, 0:N], yb[0:H1, 0, 0:N], temp[:], None, ALU.mult).then_inc(lg_done.sem, 1)
                dve.wait_ge(*lg_done.of(b))
                dve.tensor_reduce(lgm[:, 0:1], lg[:, 0:N], AX.X, ALU.max, negate=True).then_inc(lmax_done.sem, 1)

            def token_softmax(b):
                dve.wait_ge(*lexp_done.of(b))
                dve.reciprocal(lgm[:, 2:3], lgm[:, 1:2]).then_inc(pi_steps.sem, 1)
                dve.wait_ge(*pi_steps.of(b, 1))
                dve.tensor_scalar(pi[:, 0:N], lg[:, 0:N], lgm[:, 2:3], None, ALU.mult).then_inc(pi_steps.sem, 1)
                dve.wait_ge(*pi_steps.of(b, 2))
                dve.tensor_reduce(lgm[:, 3:4], pi[:, 0:N], AX.X, ALU.add).then_inc(pi_steps.sem, 1)
                dve.wait_ge(*pi_steps.of(b, 3))
                dve.tensor_scalar(lgm[:, 3:4], lgm[:, 3:4], 1e-8, None, ALU.add).then_inc(pi_steps.sem, 1)
                dve.wait_ge(*pi_steps.of(b, 4))
                dve.reciprocal(pi[:, N:NE], lgm[:, 3:4]).then_inc(pi_steps.sem, 1)
                dve.wait_ge(*pi_steps.of(b, 5))
                if not first(b):
                    dve.wait_ge(*pib_ready.before(b))
                dve.tensor_copy(pi_parts[0:H1, :], pi[:]).then_inc(pi_steps.sem, 1)
                dve.wait_ge(*pi_steps.of(b, 6))
                dve.tensor_tensor(pi_r[:], pi[:], pi_parts[0:H1, :], ALU.subtract).then_inc(pi_steps.sem, 1)

            def token_low(b):
                dve.wait_ge(*pi_mid_sig.of(b))
                dve.tensor_tensor(pi_parts[64:64 + H1, :], pi_r[:], pi_mid[:], ALU.subtract).then_inc(pi_low_done.sem, 1)

            def token_products(b, j0, j1):
                for j in range(j0, j1):
                    dve.wait_ge(*pib_ready.of(b, j + 1))
                    dve.tensor_tensor(u[:, j, :], w_s[:, j, :], yb[:, j % 2, 0:NE], ALU.mult).then_inc(u_done.sem, 1)
                    if j > 0:
                        dots_of(b, j - 1)
                if j1 == IT:
                    dots_of(b, IT - 1)

            def dots_of(b, j):
                dve.wait_ge(*u_done.of(b, j + 1))
                dve.tensor_tensor_reduce(out=junk[:, j % 2, 0:N], in0=u[:, j, 0:N], in1=w_s[:, j, 0:N], scale=1.0, scalar=0.0,
                                         op0=ALU.mult, op1=ALU.add, accum_out=dots[:, j:j + 1]).then_inc(dots_done.sem, 1)

            def scaled_weights(b):
                dve.wait_ge(*dots_done.of(b))
                dve.tensor_tensor(natt[:], dots[:], u[:, :, N], ALU.mult).then_inc(att_steps.sem, 1)
                dve.wait_ge(*att_steps.of(b, 1))
                dve.tensor_scalar(natt[:], natt[:], -1.0, -1.0, ALU.mult, ALU.add).then_inc(att_steps.sem, 1)
                dve.wait_ge(*att_steps.of(b, 2))
                dve.reciprocal(natt[:], natt[:]).then_inc(att_steps.sem, 1)
                dve.wait_ge(*att_steps.of(b, 3))
                dve.tensor_tensor(w_oa[:], w_out[:], natt[:].unsqueeze(2).to_broadcast([128, IT, D]), ALU.mult)\
                   .then_inc(woa_done.sem, 1)

            def third_norm(b):
                dve.wait_ge(*hb_done.of(b))
                for k, (t0, t1) in enumerate(((0, 2), (2, 3))):
                    dve.wait_ge(*o_ready.of(b, k + 1))
                    dve.tensor_tensor(res[:, t0:t1, :], yb[0:P, k, 0:D * (t1 - t0)].rearrange("p (t d) -> p t d", d=D),
                                      res[:, t0:t1, :], ALU.add).then_inc(h1_done.sem, 1)
                dve.wait_ge(*h1_done.of(b))
                stats(res, ln3, bn3)
                aggregate(b, ln3, bn3, ag3)
                dve.wait_ge(*ag3.of(b))
                if not first(b):
                    dve.wait_ge(*ns_ready.before(b))
                for t in range(T):
                    dve.scalar_tensor_tensor(out=nr[:, t, 0:D], in0=res[:, t, :], scalar=ln3[1][:, t, 0:1], in1=rows[:, 3, :],
                                             op0=ALU.subtract, op1=ALU.mult).then_inc(nrt_done.sem, 1)

            def third_norm_end(b):
                dve.wait_ge(*r_steps.of(b))
                if not first(b):
                    dve.wait_ge(*h2_done.before(b))
                for t in range(T):
                    dve.wait_ge(*nrt_done.of(b, t + 1))
                    dve.scalar_tensor_tensor(out=nr[:, t, 0:D], in0=nr[:, t, 0:D], scalar=r4[:, t:t + 1], in1=rows[:, 4, :],
                                             op0=ALU.mult, op1=ALU.add).then_inc(nr_done.sem, 1)
                for t in range(T):
                    dve.tensor_scalar(zed[:, t, :], res[:, t, :], ln3[1][:, t, 0:1], r3[:, t:t + 1],
                                      ALU.subtract, ALU.mult).then_inc(z_done.sem, 1)

            def scores(b):
                dve.wait_ge(*sexp_done.of(b))
                dve.tensor_scalar(sexp[:], sexp[:], 1.0, None, ALU.add).then_inc(sc_steps.sem, 1)
                dve.wait_ge(*sc_steps.of(b, 1))
                dve.reciprocal(nr[:, :, D], sexp[:]).then_inc(sc_steps.sem, 1)

            def ranks(b):
                dve.wait_ge(*sb_ready.of(b))
                if not first(b):
                    dve.wait_ge(*rk_ready.before(b))
                for t in range(T):
                    dve.scalar_tensor_tensor(out=eqm[:, t, 0:N], in0=zb[0:P, 2, 0:N], scalar=nr[:, t, D:D + 1], in1=later[:, t, :],
                                             op0=ALU.is_equal, op1=ALU.mult).then_inc(eq_done.sem, 1)
                for t in range(T):
                    dve.wait_ge(*eq_done.of(b, t + 1))
                    dve.scalar_tensor_tensor(out=less[:, t, 0:N], in0=zb[0:P, 2, 0:N], scalar=nr[:, t, D:D + 1], in1=eqm[:, t, 0:N],
                                             op0=ALU.is_gt, op1=ALU.add).then_inc(less_done.sem, 1)

            def pooled_tokens(b):
                dve.wait_ge(*pl_ready.of(b))
                dve.tensor_scalar(pl_s[:], zb[0:C, 1, 2:3], 1e-6, None, ALU.add).then_inc(pl_steps.sem, 1)
                dve.wait_ge(*pl_steps.of(b, 1))
                dve.reciprocal(pl_r[:], pl_s[:]).then_inc(pl_steps.sem, 1)
                dve.wait_ge(*pl_steps.of(b, 2))
                dve.tensor_scalar(pl[:], zb[0:C, 1, 0:CT], pl_r[:], None, ALU.mult).then_inc(pl_steps.sem, 1)

            def slots(b):
                dve.wait_ge(*rk_ready.of(b))
                if not first(b):
                    dve.wait_ge(*mix_ready.before(b))
                dve.tensor_scalar(putT[:, 0:N], zb[0:Q, 3, 0:N], slot[:], None, ALU.is_equal).then_inc(putT_done.sem, 1)

            def queries(b):
                dve.wait_ge(*q_ready.of(b))
                if not first(b):
                    dve.wait_ge(*ql_ready.before(b))
                for c in range(CT):
                    ins = dve.tensor_tensor(qb[:, c, :, :], zb[0:C, 3, Q * c:Q * c + Q].unsqueeze(1).to_broadcast([C, H1 // 2, Q]),
                                            q_mask[:].unsqueeze(2).to_broadcast([C, H1 // 2, Q]), ALU.mult)
                ins.then_inc(qb_done.sem, 1)

            def attention_max(b, j):
                dve.wait_ge(*ql_ready.of(b, j + 1))
                if j == 0 and not first(b):
                    dve.wait_ge(*prob_done.before(b))
                dve.tensor_reduce(nmax[:, j:j + 1], zb[:, j % 2, 0:N], AX.X, ALU.max, negate=True).then_inc(qmax_done.sem, 1)

            def attention_sum(b):
                dve.wait_ge(*prob_done.of(b))
                dve.reciprocal(rsum_p[:], psum_p[:]).then_inc(rsum_done.sem, 1)
                dve.wait_ge(*rsum_done.of(b))
                dve.wait_ge(*pv_ready.of(b))
                if not first(b):
                    dve.wait_ge(*cxT_ready.before(b))
                cv = cx[:].rearrange("q (j a d) -> q j a d", j=IT, a=2)
                pv = zb[:, 0, 0:IT * 32].rearrange("q (j a d) -> q j a d", j=IT, a=2)
                dve.tensor_tensor(cv[:, :, 0, :], pv[0:Q, :, 0, :], rsum_p[0:Q, :].unsqueeze(2).to_broadcast([Q, IT, 16]), ALU.mult)
                dve.tensor_tensor(cv[:, :, 1, :], pv[Q:2 * Q, :, 1, :],
                                  rsum_p[Q:2 * Q, :].unsqueeze(2).to_broadcast([Q, IT, 16]), ALU.mult).then_inc(cx_done.sem, 1)

            def attention_out(b):
                dve.wait_ge(*ao_ready.of(b))
                dve.wait_ge(*ms_done.of(b))
                if not first(b):
                    dve.wait_ge(*mix_ready.before(b))
                dve.tensor_tensor(att[:], zb[0:Q, 1, 0:D], msel[:], ALU.subtract).then_inc(att_done.sem, 1)

            def fifth_norm(b):
                if not first(b):
                    dve.wait_ge(*h12_done.before(b))
                dve.wait_ge(*z_done.of(b))
                for k, (t0, t1) in enumerate(((0, 2), (2, 3))):
                    dve.wait_ge(*mix_ready.of(b, k + 1))
                    dve.tensor_tensor(h2[:, t0:t1, :], zb[0:P, 2 + k, 0:D * (t1 - t0)].rearrange("p (t d) -> p t d", d=D),
                                      zed[:, t0:t1, :], ALU.add).then_inc(h2_done.sem, 1)
                dve.wait_ge(*h2_done.of(b))
                stats(h2, ln5, bn5)
                aggregate(b, ln5, bn5, ag5)
                dve.wait_ge(*ag5.of(b))
                if not first(b):
                    dve.wait_ge(*n2T_ready.before(b))
                for t in range(T):
                    dve.scalar_tensor_tensor(out=n2[:, t, :], in0=h2[:, t, :], scalar=ln5[1][:, t, 0:1], in1=rows[:, 5, :],
                                             op0=ALU.subtract, op1=ALU.mult).then_inc(n2t_done.sem, 1)

            def fifth_norm_end(b):
                dve.wait_ge(*rs5.of(b))
                for t in range(T):
                    dve.wait_ge(*n2t_done.of(b, t + 1))
                    dve.scalar_tensor_tensor(out=n2[:, t, :], in0=n2[:, t, :], scalar=ln5[3][:, t:t + 1], in1=rows[:, 6, :],
                                             op0=ALU.mult, op1=ALU.add).then_inc(n2_done.sem, 1)

            def result(b):
                dve.wait_ge(*h12_done.of(b))
                if not first(b):
                    dve.wait_ge(*stored.before(b))
                for i, (t0, t1) in enumerate(((0, 2), (2, 3))):
                    dve.wait_ge(*w2_ready.of(b, i + 1))
                    dve.tensor_tensor(y_out[:, t0:t1, :], zb[0:P, 2 + i, 0:D * (t1 - t0)].rearrange("p (t d) -> p t d", d=D),
                                      res_q[:, t0:t1, :], ALU.add).then_inc(y_done.sem, 1)

            def step(p, q, w):
                front, back = p is not None, q is not None
                if front:
                    pool_pairs(p)
                if back:
                    scores(q)
                depthwise(w, 0, 1)
                if back:
                    ranks(q)
                    pooled_tokens(q)
                depthwise(w, 1, 2)
                if front:
                    spectrum_stats(p)
                if back:
                    slots(q)
                if front:
                    spectrum_norm(p)
                depthwise(w, 2, 3)
                if back:
                    queries(q)
                if front:
                    second_norm(p)
                for j in range(IT):
                    if back:
                        attention_max(q, j)
                    if j in (1, 3, 5):
                        depthwise(w, 3 + j // 2, 4 + j // 2)
                if first(p):
                    dve.wait_ge(rest_in.sem, REST)
                    dve.tensor_copy(head_sel[:], head_sel32[:]).then_inc(consts.sem, 1)
                if front:
                    token_norms(p)
                if back:
                    attention_sum(q)
                if front:
                    token_max(p)
                if back:
                    attention_out(q)
                if front:
                    token_softmax(p)
                depthwise(w, 6, 7)
                if front:
                    token_low(p)
                if back:
                    fifth_norm(q)
                if front:
                    token_products(p, 0, 3)
                if back:
                    fifth_norm_end(q)
                if front:
                    token_products(p, 3, 6)
                    scaled_weights(p)
                    third_norm(p)
                if back:
                    result(q)
                if front:
                    third_norm_end(p)

            depthwise(0, 0, K)
            pipeline(dve, step)

        @block.gpsimd
        def _(pool):
            pool.memset(eps3[:], EPS).then_inc(consts.sem, 1)
            pool.memset(half3[:], -0.5).then_inc(consts.sem, 1)
            pool.wait_ge(consts.sem, 6)
            pool.wait_ge(fft_in.sem, FFT)

            def rstd(b, buffers, ag, ve, rs):
                pool.wait_ge(*ag.of(b))
                pool.tensor_tensor(buffers[2][:], buffers[1][:, :, 1], eps3[:], ALU.add).then_inc(ve.sem, 1)
                pool.wait_ge(*ve.of(b))
                pool.tensor_tensor(buffers[3][:], buffers[2][:], half3[:], ALU.pow).then_inc(rs.sem, 1)

            def step(p, q, w):
                front, back = p is not None, q is not None
                if front:
                    rstd(p, ln1, ag1, ve1, rs1)
                    rstd(p, ln2, ag2, ve2, rs2)
                    pool.wait_ge(*xh_done.of(p))
                    pool.tensor_tensor(res[:], res[:], rows[:, 2:3, :].to_broadcast([P, T, D]), ALU.add).then_inc(hb_done.sem, 1)
                if back:
                    rstd(q, ln5, ag5, ve5, rs5)
                    pool.wait_ge(*h2_done.of(q))
                    pool.wait_ge(*hz_done.of(q))
                    pool.tensor_tensor(res_q[:], res_q[:], h2[:], ALU.add).then_inc(h12_done.sem, 1)
                if front:
                    pool.wait_ge(*ag3.of(p))
                    var = ln3[1][:, :, 1]
                    for i, (o, a, c, op) in enumerate(((ln3[2], var, eps3[:], ALU.add), (r3, ln3[2][:], half3[:], ALU.pow),
                                                       (r4a, r3[:], r3[:], ALU.mult), (r4b, r4a[:], var, ALU.mult),
                                                       (r4c, r4b[:], eps3[:], ALU.add), (r4b, r4c[:], half3[:], ALU.pow),
                                                       (r4, r4b[:], r3[:], ALU.mult))):
                        if i:
                            pool.wait_ge(*r_steps.of(p, i))
                        pool.tensor_tensor(o[:], a, c, op).then_inc(r_steps.sem, 1)
                    pool.wait_ge(*h1_done.of(p))
                    if not first(p):
                        pool.wait_ge(*y_done.before(p))
                    pool.tensor_tensor(res_q[:], res[:], rows[:, 7:8, :].to_broadcast([P, T, D]), ALU.add).then_inc(hz_done.sem, 1)

            pipeline(pool, step)

        @block.scalar
        def _(act):
            for dst, name in rests:
                act.dma_start(dst if isinstance(dst, bass.AP) else dst[:], dram[name]).then_inc(rest_in.sem, 16)

            def relu(b):
                if not first(b):
                    act.wait_ge(*pool_done.before(b))
                for t in range(T):
                    act.wait_ge(*pw_ready.of(b, t + 1))
                    src = (xb[0:P, 0], xb[0:P, 1], yb[0:P, 0])[t]
                    act.activation(even[:, t, :], src[:, 0:D], ACT.Relu).then_inc(relu_done.sem, 1)

            def spectrum_parts(b):
                act.wait_ge(*fa_ready.of(b))
                if not first(b):
                    act.wait_ge(*y_ready.before(b))
                act.activation(fc[:, :, 0:KF], xb[0:C, :, 0:KF], ACT.Copy)
                act.activation(fs[:, :, 0:KF], xb[0:C, :, KF:2 * KF], ACT.Copy)
                act.activation(fc[:, :, KF:N], xb[0:C, :, KF - 1:0:-1], ACT.Copy)
                act.activation(fs[:, :, KF:N], xb[0:C, :, 2 * KF - 1:KF:-1], ACT.Copy, scale=-1.0).then_inc(fcs_done.sem, 1)

            def front_input(b):
                act.wait_ge(*xhT_ready.of(b))
                if not first(b):
                    act.wait_ge(*qkv_ready.before(b))
                act.activation(xhT[:, :, 0:N], xb[0:C, :, 0:N], ACT.Copy).then_inc(xhT_done.sem, 1)
                if first(b):
                    act.wait_ge(rest_in.sem, REST)
                    act.wait_ge(consts.sem, 6)

            def squares(b, j):
                act.wait_ge(*qkv_ready.of(b, j + 1))
                if j == 0 and not first(b):
                    act.wait_ge(*dots_done.before(b))
                    act.wait_ge(*o_ready.before(b))
                act.activation(w_s[:, j, 0:N], yb[:, j % 2, 0:N], ACT.Copy)
                act.activation(w_sq[:, j, 0:N], yb[:, j % 2, 0:N], ACT.Square, accum_out=nrm[:, j:j + 1]).then_inc(sq_done.sem, 1)

            def token_exp(b):
                act.wait_ge(*lmax_done.of(b))
                act.activation(lg[:, 0:N], lg[:, 0:N], ACT.Exp, bias=lgm[:, 0:1], accum_out=lgm[:, 1:2]).then_inc(lexp_done.sem, 1)

            def token_mid(b):
                act.wait_ge(*pi_steps.of(b, 7))
                act.activation(pi_mid[:], pi_r[:], ACT.Copy).then_inc(pi_mid0.sem, 1)
                act.wait_ge(*pi_mid0.of(b))
                act.activation(pi_parts[32:32 + H1, :], pi_mid[:], ACT.Copy).then_inc(pi_mid_sig.sem, 1)

            def routed_input(b):
                act.wait_ge(*nT_ready.of(b))
                if not first(b):
                    act.wait_ge(*mix_ready.before(b))
                act.activation(nT[0:C, :, 0:N], zb[0:C, 0:2, 0:N], ACT.Copy).then_inc(nT_done.sem, 1)

            def keys_values(b):
                act.wait_ge(*k_ready.of(b))
                if not first(b):
                    act.wait_ge(*ql_ready.before(b))
                for c in range(CT):
                    ins = act.activation(kT[:, c, 0:N], zb[0:C, 2 + c, 0:N], ACT.Identity, bias=b_k[:, c:c + 1])
                ins.then_inc(kT_done.sem, 1)
                for k, (t0, t1) in enumerate(((0, 2), (2, 3))):
                    src = zb[0:P, k, 0:(D + 1) * (t1 - t0)].rearrange("p (t d) -> p t d", d=D + 1)
                    act.wait_ge(*v_ready.of(b, k + 1))
                    if k == 0 and not first(b):
                        act.wait_ge(*pv_ready.before(b))
                    act.activation(sexp[:, t0:t1], src[:, :, D], ACT.Exp, scale=-1.0).then_inc(sexp_done.sem, 1)
                for k, (t0, t1) in enumerate(((0, 2), (2, 3))):
                    src = zb[0:P, k, 0:(D + 1) * (t1 - t0)].rearrange("p (t d) -> p t d", d=D + 1)
                    act.activation(v[:, t0:t1, :], src[:, :, 0:D], ACT.Copy).then_inc(v_done.sem, 1)

            def score_row(b):
                act.wait_ge(*less_done.of(b))
                act.activation(nT[C:C + 1, 1, 0:N], zb[C:C + 1, 2, 0:N], ACT.Copy).then_inc(sc_row_done.sem, 1)

            def pooled_row(b):
                act.wait_ge(*pwm_ready.of(b))
                act.activation(w_m[C:C + 1, 1, :], zb[0:1, 1, 64:64 + D], ACT.Copy).then_inc(pwm_done.sem, 1)

            def slots(b):
                act.wait_ge(*put_ready.of(b))
                act.activation(put[:], zb[0:P, 0, 0:T * Q].rearrange("p (t q) -> p t q", q=Q), ACT.Copy).then_inc(put_done.sem, 1)

            def selected(b):
                act.wait_ge(*ns_ready.of(b))
                act.activation(nsT[0:C, 0, :], zb[0:C, 2, 0:Q], ACT.Copy)
                act.activation(nsT[:, 1, :], zb[0:C + 1, 2, Q:2 * Q], ACT.Copy).then_inc(ns_done.sem, 1)

            def selected_mix(b):
                act.wait_ge(*ms_ready.of(b))
                if not first(b):
                    act.wait_ge(*att_done.before(b))
                act.activation(msel[:], zb[0:Q, 1, 0:D], ACT.Copy).then_inc(ms_done.sem, 1)

            def exponentials(b, j):
                act.wait_ge(*qmax_done.of(b, j + 1))
                if j == 0 and not first(b):
                    act.wait_ge(*w2_ready.before(b))
                    act.wait_ge(*rsum_done.before(b))
                act.activation(probs[:, j, 0:N], zb[:, j % 2, 0:N], ACT.Exp, bias=nmax[:, j:j + 1],
                               accum_out=psum_p[:, j:j + 1]).then_inc(prob_done.sem, 1)

            def turned(b, j):
                act.wait_ge(*prT_ready.of(b, j + 1))
                act.activation(probsT[:, j, :, :], zb[0:P, 2 + j % 2, 0:T * 128].rearrange("p (t q) -> p t q", q=128),
                               ACT.Copy).then_inc(prT_done.sem, 1)

            def context(b):
                act.wait_ge(*cxT_ready.of(b))
                act.activation(cxT[0:C, :, :], zb[0:C, 0, 0:2 * Q].rearrange("p (c q) -> p c q", q=Q), ACT.Copy).then_inc(cxT_done.sem, 1)

            def forward_input(b):
                act.wait_ge(*n2T_ready.of(b))
                if not first(b):
                    act.wait_ge(*w1_ready.before(b))
                act.activation(n2T[:, :, 0:N], zb[0:C, 0:2, 0:N], ACT.Copy).then_inc(n2T_done.sem, 1)

            def gelus(b, j):
                act.wait_ge(*w1_ready.of(b, j + 1))
                act.activation(gelu[:, j, 0:N], zb[:, j % 2, 0:N], ACT.Gelu, bias=b_1[:, j:j + 1]).then_inc(gelu_done.sem, 1)

            def step(p, q, w):
                front, back = p is not None, q is not None
                if front:
                    relu(p)
                if back:
                    routed_input(q)
                    keys_values(q)
                if front:
                    spectrum_parts(p)
                if back:
                    score_row(q)
                    pooled_row(q)
                    slots(q)
                    selected(q)
                    selected_mix(q)
                if front:
                    front_input(p)
                for j in range(IT):
                    if front:
                        squares(p, j)
                    if back:
                        exponentials(q, j)
                        if j:
                            turned(q, j - 1)
                if back:
                    turned(q, IT - 1)
                    context(q)
                if front:
                    token_exp(p)
                    token_mid(p)
                if back:
                    forward_input(q)
                    for j in range(IT):
                        gelus(q, j)

            pipeline(act, step)

        @block.tensor
        def _(pe):
            mm = pe.matmul

            def transposes(src, dst):
                for c in range(CT):
                    for t in range(T):
                        ins = pe.transpose(dst[0:C, c, tok(t)], src[:, t, chan(c)], ident[0:P, 0:P])
                return ins

            pe.wait_ge(first_in.sem, FIRST)

            def pointwise(b):
                pe.wait_ge(*dw_done.of(b))
                if not first(b):
                    pe.wait_ge(*xhT_done.before(b))
                for t in range(T):
                    if t == 2 and not first(b):
                        pe.wait_ge(*h1_done.before(b))
                    bank = (xb[0:P, 0], xb[0:P, 1], yb[0:P, 0])[t]
                    for e in range(2):
                        f0 = 2 * P * t + e
                        o = bank[:, D * e:D * e + D]
                        mm(o, dw[0:C + 1, 0, f0:f0 + 2 * P - 1:2], w_pw[:, 0, :], start=True, stop=False)
                        ins = mm(o, dw[0:C, 1, f0:f0 + 2 * P - 1:2], w_pw[0:C, 1, :], start=False, stop=True)
                    ins.then_inc(pw_ready.sem, 1)

            def over_tokens(b):
                if first(b):
                    pe.wait_ge(fft_in.sem, FFT)
                pe.wait_ge(*pool_done.of(b))
                for c in range(CT):
                    for t in range(T):
                        ins = mm(xb[0:C, c, 0:2 * KF], pooled_h[:, t, chan(c)], dft_n[:, t, :], start=(t == 0), stop=(t == T - 1))
                ins.then_inc(fa_ready.sem, 1)

            def over_channels(b):
                pe.wait_ge(*fcs_done.of(b))
                for t in range(T):
                    o = xb[0:P, t // 2, D * (t % 2):D * (t % 2) + D]
                    for i, (f, r) in enumerate(((fc, 0), (fs, 1))):
                        for c in range(CT):
                            ins = mm(o, f[:, c, tok(t)], dft_d[:, r, c, :], start=(i + c == 0), stop=(i + c == 2))
                    if t:
                        ins.then_inc(y_ready.sem, 1)

            def front_input(b):
                pe.wait_ge(*xh_done.of(b))
                transposes(xh, xb).then_inc(xhT_ready.sem, 1)

            def qkv(b, j):
                if j == 0:
                    pe.wait_ge(*xhT_done.of(b))
                if j >= 2:
                    pe.wait_ge(*sq_done.of(b, j - 1))
                for c in range(CT):
                    ins = mm(yb[:, j % 2, 0:N], w_qkv[:, c, 128 * j:128 * j + 128], xhT[:, c, 0:N], start=(c == 0), stop=(c == 1))
                ins.then_inc(qkv_ready.sem, 1)

            def token_logits(b):
                pe.wait_ge(*rhead_done.of(b))
                for j in range(IT):
                    ins = mm(yb[0:H1, 0, 0:N], rhead[:, j, :], w_sq[:, j, 0:N], start=(j == 0), stop=(j == IT - 1))
                ins.then_inc(lg_ready.sem, 1)

            def spread(b, j):
                if j == 0:
                    if first(b):
                        pe.wait_ge(consts.sem, 7)
                    pe.wait_ge(*pi_low_done.of(b))
                if j >= 2:
                    pe.wait_ge(*u_done.of(b, j - 1))
                mm(yb[:, j % 2, 0:NE], head_sel[:, j, :], pi_parts[:], start=True, stop=True).then_inc(pib_ready.sem, 1)

            def token_out(b):
                pe.wait_ge(*woa_done.of(b))
                for t in range(T):
                    o = yb[0:P, t // 2, D * (t % 2):D * (t % 2) + D]
                    for j in range(IT):
                        ins = mm(o, u[:, j, tok(t)], w_oa[:, j, :], start=(j == 0), stop=(j == IT - 1))
                    if t:
                        ins.then_inc(o_ready.sem, 1)

            def routed_input(b):
                pe.wait_ge(*nr_done.of(b))
                if not first(b):
                    pe.wait_ge(*gelu_done.before(b))
                transposes(nr, zb).then_inc(nT_ready.sem, 1)

            def keys_values(b):
                pe.wait_ge(*nT_done.of(b))
                if not first(b):
                    pe.wait_ge(*y_done.before(b))
                for k in range(CT):
                    for c in range(CT):
                        ins = mm(zb[0:C, 2 + k, 0:N], w_k[:, c, chan(k)], nT[0:C, c, 0:N], start=(c == 0), stop=(c == 1))
                ins.then_inc(k_ready.sem, 1)
                for t in range(T):
                    o = zb[0:P, t // 2, (D + 1) * (t % 2):(D + 1) * (t % 2) + D + 1]
                    mm(o, nT[:, 0, tok(t)], w_v[:, 0, :], start=True, stop=False)
                    ins = mm(o, nT[0:C, 1, tok(t)], w_v[0:C, 1, :], start=False, stop=True)
                    if t:
                        ins.then_inc(v_ready.sem, 1)

            def score_sums(b):
                pe.wait_ge(*kT_done.of(b))
                pe.wait_ge(*sc_steps.of(b))
                for t in range(T):
                    ins = pe.transpose(zb[0:P, 2, tok(t)], nr[:, t, D:D + 1].to_broadcast([P, P]), ident[0:P, 0:P])
                ins.then_inc(sb_ready.sem, 1)
                pe.wait_ge(*v_done.of(b))
                for c in range(CT + 1):
                    for t in range(T):
                        lhs = ones[:] if c == CT else nr[:, t, chan(c)]
                        ins = mm(zb[0:C, 1, c:c + 1], lhs, nr[:, t, D:D + 1], start=(t == 0), stop=(t == T - 1))
                ins.then_inc(pl_ready.sem, 1)

            def pooled_row(b):
                pe.wait_ge(*pl_steps.of(b))
                for c in range(CT):
                    ins = mm(zb[0:1, 1, 64:64 + D], pl[:, c:c + 1], w_m[0:C, c, :], start=(c == 0), stop=(c == 1))
                ins.then_inc(pwm_ready.sem, 1)

            def ranks(b):
                pe.wait_ge(*less_done.of(b))
                for t in range(T):
                    ins = mm(zb[0:Q, 3, 0:N], ones_bf[:], less[:, t, 0:N], start=(t == 0), stop=(t == T - 1))
                ins.then_inc(rk_ready.sem, 1)

            def slots(b):
                pe.wait_ge(*putT_done.of(b))
                for t in range(T):
                    ins = mm(zb[0:P, 0, Q * t:Q * t + Q], putT[:, tok(t)], ident[0:Q, 0:Q], start=True, stop=True)
                ins.then_inc(put_ready.sem, 1)

            def selected(b):
                pe.wait_ge(*sc_row_done.of(b))
                pe.wait_ge(*put_done.of(b))
                for c in range(CT):
                    cols = chan(0) if c == 0 else slice(C, D + 1)
                    for t in range(T):
                        ins = mm(zb[0:C + c, 2, Q * c:Q * c + Q], nr[:, t, cols], put[:, t, :], start=(t == 0), stop=(t == T - 1))
                ins.then_inc(ns_ready.sem, 1)

            def selected_products(b):
                pe.wait_ge(*ns_done.of(b))
                for k in range(CT):
                    o = zb[0:C, 3, Q * k:Q * k + Q]
                    mm(o, w_q[:, 0, chan(k)], nsT[:, 0, :], start=True, stop=False)
                    ins = mm(o, w_q[0:C, 1, chan(k)], nsT[0:C, 1, :], start=False, stop=True)
                ins.then_inc(q_ready.sem, 1)
                pe.wait_ge(*pwm_done.of(b))
                for c in range(CT):
                    ins = mm(zb[0:Q, 1, 0:D], nsT[:, c, :], w_m[:, c, :], start=(c == 0), stop=(c == 1))
                ins.then_inc(ms_ready.sem, 1)

            def logits(b, j):
                if j == 0:
                    pe.wait_ge(*qb_done.of(b))
                if j == 1:
                    pe.wait_ge(*ms_done.of(b))
                if j >= 2:
                    pe.wait_ge(*prob_done.of(b, j - 1))
                c, i = divmod(j, 3)
                mm(zb[:, j % 2, 0:N], qb[:, c, 2 * i:2 * i + 2, :].rearrange("p h q -> p (h q)"), kT[:, c, 0:N],
                   start=True, stop=True).then_inc(ql_ready.sem, 1)

            def turn(b, j):
                if j >= 2:
                    pe.wait_ge(*prT_done.of(b, j - 1))
                pe.wait_ge(*prob_done.of(b, j + 1))
                for t in range(T):
                    ins = pe.transpose(zb[0:P, 2 + j % 2, 128 * t:128 * t + 128], probs[:, j, tok(t)], ident[:])
                ins.then_inc(prT_ready.sem, 1)

            def values(b):
                for j in range(IT):
                    pe.wait_ge(*prT_done.of(b, j + 1))
                    for t in range(T):
                        ins = mm(zb[:, 0, 32 * j:32 * j + 32], probsT[:, j, t, :], v[:, t, 32 * j:32 * j + 32],
                                 start=(t == 0), stop=(t == T - 1))
                ins.then_inc(pv_ready.sem, 1)

            def context(b):
                pe.wait_ge(*cx_done.of(b))
                for c in range(CT):
                    ins = mm(zb[0:C, 0, Q * c:Q * c + Q], cx[:, chan(c)], ident[0:Q, 0:Q], start=True, stop=True)
                ins.then_inc(cxT_ready.sem, 1)

            def attention_out(b):
                pe.wait_ge(*cxT_done.of(b))
                mm(zb[0:Q, 1, 0:D], cxT[:, 0, :], w_o[:, 0, :], start=True, stop=False)
                mm(zb[0:Q, 1, 0:D], cxT[0:C, 1, :], w_o[0:C, 1, :], start=False, stop=True).then_inc(ao_ready.sem, 1)

            def merged(b):
                pe.wait_ge(*att_done.of(b))
                for t in range(T):
                    o = zb[0:P, 2 + t // 2, D * (t % 2):D * (t % 2) + D]
                    for c in range(CT):
                        mm(o, nT[:, c, tok(t)], w_m[:, c, :], start=(c == 0), stop=False)
                    ins = mm(o, putT[:, tok(t)], att[:], start=False, stop=True)
                    if t:
                        ins.then_inc(mix_ready.sem, 1)

            def forward_input(b):
                pe.wait_ge(*n2_done.of(b))
                transposes(n2, zb).then_inc(n2T_ready.sem, 1)

            def forward_up(b, j):
                if j == 0:
                    pe.wait_ge(*n2T_done.of(b))
                if j >= 2:
                    pe.wait_ge(*gelu_done.of(b, j - 1))
                for c in range(CT):
                    ins = mm(zb[:, j % 2, 0:N], w_1[:, c, 128 * j:128 * j + 128], n2T[:, c, 0:N], start=(c == 0), stop=(c == 1))
                ins.then_inc(w1_ready.sem, 1)

            def forward_down(b):
                pe.wait_ge(*gelu_done.of(b))
                for t in range(T):
                    o = zb[0:P, 2 + t // 2, D * (t % 2):D * (t % 2) + D]
                    for j in range(IT):
                        ins = mm(o, gelu[:, j, tok(t)], w_2[:, j, :], start=(j == 0), stop=(j == IT - 1))
                    if t:
                        ins.then_inc(w2_ready.sem, 1)

            def step(p, q, w):
                front, back = p is not None, q is not None
                if front:
                    pointwise(p)
                if back:
                    routed_input(q)
                    keys_values(q)
                if front:
                    over_tokens(p)
                if back:
                    score_sums(q)
                if front:
                    over_channels(p)
                if back:
                    pooled_row(q)
                    ranks(q)
                    slots(q)
                    selected(q)
                    selected_products(q)
                if front:
                    front_input(p)
                for j in range(IT):
                    if front:
                        qkv(p, j)
                    if back:
                        logits(q, j)
                        if j:
                            turn(q, j - 1)
                if back:
                    turn(q, IT - 1)
                    values(q)
                if front:
                    token_logits(p)
                if back:
                    context(q)
                    attention_out(q)
                    merged(q)
                if front:
                    spread(p, 0)
                    spread(p, 1)
                    spread(p, 2)
                if back:
                    forward_input(q)
                for j in range(IT):
                    if front and j >= 3:
                        spread(p, j)
                    if back:
                        forward_up(q, j)
                if front:
                    token_out(p)
                if back:
                    forward_down(q)

            pipeline(pe, step)


def kernel(**inputs):
    import numpy as np
    import concourse.bacc as bacc
    from concourse.bass_utils import run_bass_kernel_spmd as run

    f = np.float32
    a = {k: np.asarray(v) for k, v in inputs.items()}

    def tiles(w, p):
        return np.ascontiguousarray(w.reshape(-1, p, w.shape[-1]).transpose(1, 0, 2))

    def with_row(w, row):
        extra = np.stack([row, np.zeros_like(row)])[None]
        return np.concatenate([tiles(w, C), extra], 0)

    x = np.zeros((B, CT, C, S + 6), f)
    x[:, :, :, 3:3 + S] = a["x"].transpose(0, 2, 1).reshape(B, CT, C, S)
    n, k, d = np.arange(N), np.arange(KF), np.arange(D)
    turn_n = 2 * np.pi * ((n[:, None] * k) % N) / N
    turn_d = 2 * np.pi * ((d[:, None] * d) % D) / D
    p128, q = np.arange(128), np.arange(Q)
    head = 2 * np.arange(IT)[None, :] + (p128 // 64)[:, None]
    sel = np.zeros((96, IT, 128), f)
    for r in (0, 32, 64):
        sel[r:r + H1] = (head.T[None] == np.arange(H1)[:, None, None])
    m = (P * np.arange(T)[None, :] + np.arange(P)[:, None])[:, :, None]
    data = {
        "x": np.ascontiguousarray(x.transpose(0, 2, 1, 3)),
        "w_dw": tiles(np.concatenate([a["L0_tok_w_dw"][:, 0], a["L0_tok_b_dw"][:, None]], 1), C),
        "w_pw": with_row(a["L0_tok_w_pw"][:, :, 0].T, a["L0_tok_b_pw"]),
        "ones_row": np.ones((1, S), f),
        "dft_n": tiles(np.concatenate([np.cos(turn_n), np.sin(turn_n)], 1), P).astype(f),
        "dft_d": np.stack([tiles(np.cos(turn_d), C), tiles(-np.sin(turn_d), C)], 1).astype(f),
        "rows": np.broadcast_to(np.stack([a["L0_tok_gamma"], a["L0_tok_beta"], a["L0_attn_b_out"], a["L0_ffn_g1"], a["L0_ffn_b1"],
                                          a["L0_ffn_g2"], a["L0_ffn_b2"], a["L0_ffn_bf2"]]), (P, 8, D)),
        "ident": np.eye(128, dtype=f),
        "w_qkv": tiles(a["L0_attn_w_qkv"], C),
        "temp": a["L0_attn_temp"],
        "head_mask": (head[:, :, None] == np.arange(H1)).astype(f),
        "head_sel": sel,
        "w_out": tiles(a["L0_attn_w_out"], 128),
        "w_k": tiles(a["L0_ffn_Wk"], C),
        "b_k": a["L0_ffn_bk"].reshape(CT, C).T,
        "w_v": with_row(np.concatenate([a["L0_ffn_Wv"], a["L0_ffn_Wr"][:, None]], 1),
                        np.concatenate([a["L0_ffn_bv"], a["L0_ffn_br"].reshape(1)])),
        "w_q": with_row(a["L0_ffn_Wq"], a["L0_ffn_bq"]),
        "w_o": with_row(a["L0_ffn_Wo"], a["L0_ffn_bo"]),
        "w_m": with_row(a["L0_ffn_Wm"], a["L0_ffn_bm"]),
        "q_mask": 0.25 * (np.arange(C)[:, None] // 16 == np.arange(H1 // 2)).astype(f),
        "later": (n[None, None, :] > m).astype(f),
        "slot": np.where(q < SEL, q, -1).astype(f)[:, None],
        "w_1": tiles(a["L0_ffn_W1"], C),
        "b_1": a["L0_ffn_bf1"].reshape(IT, 128).T,
        "w_2": tiles(a["L0_ffn_W2"], 128),
        "ones_n": np.ones((1, N), f), "ones_q": np.ones((1, Q), f), "ones_q2": np.ones((1, Q), f),
    }
    nc = bacc.Bacc("TRN2", target_bir_lowering=False, num_devices=1)
    arrays, dram = {}, {}
    for name, value in data.items():
        value = np.ascontiguousarray(value)
        assert value.dtype == f, name
        arrays[f"in_{name}"] = value
        dram[name] = nc.dram_tensor(f"in_{name}", value.shape, mybir.dt.float32, kind="ExternalInput").ap()
    out = nc.dram_tensor("out_0", (B, N, D), mybir.dt.float32, kind="ExternalOutput").ap()
    audio_tower(nc, dram, out)
    result = run(nc, [arrays], core_ids=[0])
    return result.results[0]["out_0"]
```

```python
import concourse.bass as bass
from concourse import mybir
from contextlib import ExitStack

B, S, D, K = 8, 750, 192, 7
N = S // 2
P, T = 125, 3
C, CT = 96, 2
H1, IT = 12, 6
KF = N // 2 + 1
KL = D // 2 + 1
DV = D + 2
NE = N + 1
SEL = int(round(0.15 * N))
Q = 64
EPS = 1e-5


class Signal:

    def __init__(self, sem, per_batch):
        self.sem, self.per_batch = sem, per_batch

    def of(self, b, j=None):
        return self.sem, b * self.per_batch + (self.per_batch if j is None else j)

    def before(self, b, j=None):
        j = self.per_batch if j is None else j
        return self.sem, b * self.per_batch + (j - self.per_batch)


def audio_tower(nc, dram, out):
    fp32, bf16, fp32r = mybir.dt.float32, mybir.dt.bfloat16, mybir.dt.float32r
    ALU, ACT, AX = mybir.AluOpType, mybir.ActivationFunctionType, mybir.AxisListType

    with ExitStack() as ctx:
        def sb(name, shape, dt=fp32):
            return ctx.enter_context(nc.sbuf_tensor(name, shape, dt))

        def signal(name, per_batch=1):
            return Signal(ctx.enter_context(nc.semaphore(name)), per_batch)

        x_in = sb("x_in", [C, CT, S + 6])
        w_dw = sb("w_dw_sb", [C, CT, K + 1])
        w_pw = sb("w_pw_sb", [C + 1, CT, D])
        dft_n = sb("dft_n_sb", [P, T, 2 * KF])
        dft_d = sb("dft_d_sb", [C, 2, CT, KL])
        ident = sb("ident_sb", [128, 128])
        rows = sb("rows_sb", [P, 8, D])
        w_qkv = sb("w_qkv_sb", [C, 2, CT, IT * 128], fp32r)
        temp = sb("temp_sb", [128, H1])
        head_mask = sb("head_mask_sb", [128, IT, H1])
        head_sel = sb("head_sel_sb", [64, IT, 128], fp32r)
        w_out = sb("w_out_sb", [128, IT, D])
        w_k = sb("w_k_sb", [C, 2, CT, D], fp32r)
        b_k = sb("b_k_sb", [C, CT])
        w_v = sb("w_v_sb", [C + 1, 2, CT, DV], fp32r)
        w_q = sb("w_q_sb", [C + 1, CT, D])
        w_o = sb("w_o_sb", [C + 1, CT, D])
        w_m = sb("w_m_sb", [C + 1, CT, D])
        w_mp = sb("w_mp", [C + 1, 2, CT, D], fp32r)
        q_mask = sb("q_mask_sb", [C, H1 // 2])
        later = sb("later_sb", [P, P])
        slot = sb("slot_sb", [Q, 1])
        w_1 = sb("w_1_sb", [C, 2, CT, IT * 128], fp32r)
        b_1 = sb("b_1_sb", [128, IT])
        w_2 = sb("w_2_sb", [128, 2, IT, D], fp32r)
        half3 = sb("half3", [P, 2, T])
        ones = sb("ones", [P, C])
        ones_bf = sb("ones_bf", [P, Q], bf16)

        res = sb("res", [P, T, D])
        res_q = sb("res_q", [P, T, D])
        zed = sb("zed", [P, T, D])
        n2T = sb("n2T", [C, 2, CT, NE], fp32r)

        dw = sb("dw", [C + 1, CT, S])
        even = sb("even", [P, T, D])
        pooled_h = sb("pooled_h", [P, T, D])
        scratch = sb("scratch", [128, 2, CT * NE])
        fc = scratch[0:C, 0].rearrange("c (t n) -> c t n", n=NE)
        fs = scratch[0:C, 1].rearrange("c (t n) -> c t n", n=NE)
        sines = even[:, :, 0:KL]
        xh = even
        xhT = sb("xhT", [C, 2, CT, NE], fp32r)

        def norm_buffers(n):
            return (sb(f"st{n}", [P, T, 6]), sb(f"ag{n}", [P, T, 2]), sb(f"ve{n}", [P, T]), sb(f"rs{n}", [P, T]),
                    sb(f"gate{n}", [1, 1]))

        ln1, ln2, ln3, ln5 = (norm_buffers(n) for n in (1, 2, 3, 5))

        w_s = sb("w_s", [128, IT, NE])
        w_sq = sb("w_sq", [128, IT, NE])
        nrm = sb("nrm", [128, IT])
        rnrm = sb("rnrm", [128, IT])
        rhead = sb("rhead", [128, IT, H1])
        lg = sb("lg", [H1, NE])
        lgm = sb("lgm", [H1, 4])
        pi = sb("pi", [H1, NE])
        pi_parts = sb("pi_parts", [64, NE], fp32r)
        u = w_sq
        junk = sb("junk", [128, 2, NE])
        dots = sb("dots", [128, IT])
        natt = sb("natt", [128, IT])
        w_oa = scratch[:].rearrange("p a n -> p (a n)")[:, 0:IT * D].rearrange("p (j d) -> p j d", d=D)
        ve34 = sb("ve34", [P, 2, T])
        rs34 = sb("rs34", [P, 2, T])

        nr = sb("nr", [P, T, D + 1])
        nT = sb("nT", [C + 1, 2, CT, NE], fp32r)
        kT = sb("kT", [C, CT, NE])
        v = sb("v", [P, T, D])
        sexp = sb("sexp", [P, T])
        less = sb("less", [P, T, NE], bf16)
        putT = sb("putT", [Q, NE])
        put = sb("put", [P, T, Q])
        pl_s = sb("pl_s", [C, 1])
        pl_r = sb("pl_r", [C, 1])
        pl = sb("pl", [C, CT])
        nsT = sb("nsT", [C + 1, CT, Q])
        msel = sb("msel", [Q, D])
        qb = sb("qb", [C, CT, H1 // 2, Q])
        nmax = sb("nmax", [128, IT])
        psum_p = sb("psum_p", [128, IT])
        rsum_p = sb("rsum_p", [128, IT])
        probs = sb("probs", [128, IT, NE])
        head_sel32 = probs[0:64, :, 0:128]
        w_2_32 = probs[:, :, 128:128 + D]
        w_k32 = kT[:].rearrange("c t n -> c (t n)")[:, 0:CT * D].rearrange("c (t d) -> c t d", d=D)
        w_v32 = v[0:C + 1].rearrange("c t n -> c (t n)")[:, 0:CT * (D + 1)].rearrange("c (t d) -> c t d", d=D + 1)
        probsT = sb("probsT", [P, IT, T, 128])
        cx = sb("cx", [Q, D])
        cxT = sb("cxT", [C + 1, CT, Q])
        att = sb("att", [Q, D])
        w_qkv32 = probsT[0:C].rearrange("c j t q -> c (j t q)")[:, 0:CT * IT * 128].rearrange("c (t i) -> c t i", t=CT)
        n2 = sb("n2", [P, T, D])
        h2 = sb("h2", [P, T, D])

        table_hint = sb("table_hint", [1, 1])

        gelu = sb("gelu", [128, 3, NE])
        gelu_high = sb("gelu_high", [128, IT, NE], fp32r)
        gelu_low = sb("gelu_low", [128, IT, NE], fp32r)
        res_f = sb("res_f", [P, T, D])
        y_out = res_f

        xb = ctx.enter_context(nc.psum_tensor("xb", [128, 2, 512], fp32))
        yb = ctx.enter_context(nc.psum_tensor("yb", [128, 2, 512], fp32))
        zb = ctx.enter_context(nc.psum_tensor("zb", [128, 4, 512], fp32))

        first_in = signal("first_in", 16)
        x_ready = signal("x_ready", 16)
        fft_in = signal("fft_in", 16)
        rest_in = signal("rest_in", 16)
        w_1_in = signal("w_1_in", 16)
        consts = signal("consts")
        split = signal("split")
        dw_done = signal("dw_done", CT * (K))
        pw_ready, relu_done, pool_done = signal("pw_ready", T), signal("relu_done", T), signal("pool_done", T)
        fa_ready, fcs_done = signal("fa_ready"), signal("fcs_done")
        y_ready, sines_done, spec_done = signal("y_ready", 2), signal("sines_done"), signal("spec_done")
        bn1, ag1, ve1, rs1 = signal("bn1"), signal("ag1"), signal("ve1"), signal("rs1")
        lnt_done, h0_done = signal("lnt_done", T), signal("h0_done", T)
        bn2, ag2, ve2, rs2 = signal("bn2"), signal("ag2"), signal("ve2"), signal("rs2")
        xh_done, xhT_ready, xhT_high, xhT_done = signal("xh_done", T), signal("xhT_ready"), signal("xhT_high", CT), signal("xhT_done", CT)
        qkv_ready, sq_done = signal("qkv_ready", IT), signal("sq_done", IT)
        rn1, rn2, rhead_done = signal("rn1"), signal("rn2"), signal("rhead_done")
        lg_ready, lmax_done, lexp_done = signal("lg_ready"), signal("lmax_done"), signal("lexp_done")
        pi_steps, pi_low_done = signal("pi_steps", 5), signal("pi_low_done")
        pib_ready, u_done, dots_done = signal("pib_ready", IT), signal("u_done", IT), signal("dots_done", IT)
        att_steps, woa_done, woa_act_done = signal("att_steps", 3), signal("woa_done"), signal("woa_act_done")
        o_ready = signal("o_ready", 2)
        hb_done, h1_done = signal("hb_done"), signal("h1_done", 2)
        bn3, ag3, ve3, rs3 = signal("bn3"), signal("ag3"), signal("ve3"), signal("rs3")
        z_done, nrt_done, nr_done = signal("z_done", T), signal("nrt_done", T), signal("nr_done", T)
        nT_ready, nT_high, nT_done = signal("nT_ready"), signal("nT_high"), signal("nT_done")
        sc_row_high, sc_row_done = signal("sc_row_high"), signal("sc_row_done")
        pwm_high, pwm_low = signal("pwm_high"), signal("pwm_low")
        k_ready, kT_done = signal("k_ready"), signal("kT_done")
        v_ready, v_done, sexp_done = signal("v_ready", 2), signal("v_done", 2), signal("sexp_done", 2)
        sc_steps = signal("sc_steps", 2)
        sb_ready, less_done, eq_done = signal("sb_ready"), signal("less_done", T), signal("eq_done", T)
        rk_ready, putT_done = signal("rk_ready"), signal("putT_done")
        put_ready, put_done = signal("put_ready"), signal("put_done")
        pl_ready, pl_steps, pwm_ready, pwm_done = signal("pl_ready"), signal("pl_steps", 3), signal("pwm_ready"), signal("pwm_done")
        ns_ready, ns_done = signal("ns_ready"), signal("ns_done")
        q_ready, qb_done = signal("q_ready"), signal("qb_done", CT)
        ms_ready, ms_done = signal("ms_ready"), signal("ms_done")
        ql_ready, qmax_done, prob_done = signal("ql_ready", IT), signal("qmax_done", IT), signal("prob_done", IT)
        prT_ready, prT_done = signal("prT_ready", IT), signal("prT_done", IT)
        pv_ready, rsum_done, cx_done = signal("pv_ready"), signal("rsum_done"), signal("cx_done")
        cxT_ready, cxT_done = signal("cxT_ready"), signal("cxT_done")
        ao_ready, att_done = signal("ao_ready"), signal("att_done")
        mix_ready, h2_done = signal("mix_ready", 2), signal("h2_done", 2)
        hz_done, h12_done = signal("hz_done"), signal("h12_done")
        bn5, ag5, ve5, rs5 = signal("bn5"), signal("ag5"), signal("ve5"), signal("rs5")
        n2t_done, n2_done = signal("n2t_done", T), signal("n2_done", T)
        n2T_ready, n2T_high, n2T_done = signal("n2T_ready"), signal("n2T_high"), signal("n2T_done")
        gelu_high_done, gelu_low_done = signal("gelu_high_done", IT), signal("gelu_low_done", IT)
        w1_ready, gelu_done = signal("w1_ready", IT), signal("gelu_done", IT)
        w2_ready, y_done, stored = signal("w2_ready", 2), signal("y_done", 2), signal("stored", 16)

        block = ctx.enter_context(nc.Block())

        def tok(t):
            return slice(P * t, P * (t + 1))

        def chan(c):
            return slice(C * c, C * (c + 1))

        firsts = [(w_dw, "w_dw"), (w_pw, "w_pw"), (dw[C:C + 1, 0, :], "ones_row")]
        ffts = [(dft_n, "dft_n"), (dft_d, "dft_d"), (rows, "rows"), (ident, "ident"), (w_qkv32, "w_qkv"), (temp, "temp"),
                (head_mask, "head_mask"), (head_sel32, "head_sel")]
        rests = [(w_out, "w_out"), (w_k32, "w_k"), (b_k, "b_k"), (w_v32, "w_v"), (w_q, "w_q"), (w_o, "w_o"), (w_m, "w_m"),
                 (q_mask, "q_mask"), (later, "later"), (slot, "slot"), (b_1, "b_1"), (w_2_32, "w_2"),
                 (nsT[C:C + 1, 0, :], "ones_q"), (cxT[C:C + 1, 0, :], "ones_q2")]
        MEMSETS, WEIGHTS = 5, 6
        SPLIT = MEMSETS + 2 * WEIGHTS
        FILLS, SELECTORS = 5, 6
        FIRST, FFT, REST = (16 * len(x) for x in (firsts, ffts, rests))


        def pipeline(eng, step):
            step(0, None, None, 1)
            step(1, 0, None, 2)
            step(2, 1, 0, 3)
            with eng.Fori(3, B - 1) as i:
                step(i, i - 1, i - 2, i + 1)
            step(B - 1, B - 2, B - 3, None)
            step(None, B - 1, B - 2, None)
            step(None, None, B - 1, None)

        def frames(t):
            return xb[0:P, t] if t < 2 else zb[0:P, 3]

        def first(b):
            return isinstance(b, int) and b == 0

        @block.sync
        def _(sp):
            for dst, name in firsts:
                sp.dma_start(dst if isinstance(dst, bass.AP) else dst[:], dram[name]).then_inc(first_in.sem, 16)
            sp.dma_start(x_in[:], dram["x"][0]).then_inc(x_ready.sem, 16)
            for dst, name in ffts:
                sp.dma_start(dst if isinstance(dst, bass.AP) else dst[:], dram[name]).then_inc(fft_in.sem, 16)

            sp.wait_ge(split.sem, MEMSETS + 2)
            sp.dma_start(w_qkv32, dram["w_1"]).then_inc(w_1_in.sem, 16)

            def load(b):
                sp.wait_ge(*dw_done.before(b))
                sp.dma_start(x_in[:], dram["x"][b]).then_inc(x_ready.sem, 16)

            def store(b):
                done, ring = y_done.of(b)[1], stored.before(b)[1]
                if not first(b):
                    done, ring = (v if isinstance(v, int) else sp.snap(v) for v in (done, ring))
                    sp.wait_ge(stored.sem, ring)
                sp.wait_ge(y_done.sem, done)
                sp.wait_ge(first_in.sem, FIRST)
                sp.dma_start(out[b].rearrange("(t p) d -> p t d", p=P), y_out[:]).then_inc(stored.sem, 16)

            load(1)
            load(2)
            load(3)
            load(4)
            store(0)
            with sp.Fori(3, B - 2) as i:
                load(i + 2)
                store(i - 2)
            store(B - 4)
            for b in range(B - 3, B):
                store(b)
            sp.wait_ge(*stored.of(B - 1))

        @block.vector
        def _(dve):
            dve.memset(ones[:], 1.0).then_inc(consts.sem, 1)
            dve.memset(ones_bf[:], 1.0).then_inc(consts.sem, 1)
            dve.memset(w_s[:, :, N:NE], 1.0).then_inc(consts.sem, 1)
            dve.memset(pi_parts[:].bitcast(fp32), 0.0).then_inc(consts.sem, 1)
            dve.wait_ge(first_in.sem, FIRST)

            def stats(src, buffers, bn):
                for t in range(T):
                    ins = dve.bn_stats(buffers[0][:, t, :], src[:, t, :])
                ins.then_inc(bn.sem, 1)

            def aggregate(b, buffers, bn, ag):
                dve.wait_ge(*bn.of(b))
                dve.memset(buffers[4][:], 0.0)
                for t in range(T):
                    ins = dve.bn_aggr(buffers[1][:, t, :], buffers[0][:, t, :])
                ins.then_inc(ag.sem, 1)
                dve.wait_ge(*ag.of(b))

            def plus_eps(buffers, ve):
                dve.tensor_scalar(buffers[2][:], buffers[1][:, :, 1], EPS, None, ALU.add).then_inc(ve.sem, 1)

            def depthwise(b, k0, k1):
                if b is None:
                    return
                if k0 == 0 and k1:
                    dve.wait_ge(*x_ready.of(b))
                    if not first(b):
                        dve.wait_ge(*pw_ready.before(b))
                for k in range(k0, k1):
                    for c in range(CT):
                        src = x_in[:, c, k:k + S]
                        if k == 0:
                            ins = dve.tensor_scalar(dw[0:C, c, :], src, w_dw[:, c, 0:1], w_dw[:, c, K:K + 1], ALU.mult, ALU.add)
                        else:
                            dve.wait_ge(*dw_done.of(b, CT * (k - 1) + c + 1))
                            ins = dve.scalar_tensor_tensor(out=dw[0:C, c, :], in0=src, scalar=w_dw[:, c, k:k + 1],
                                                           in1=dw[0:C, c, :], op0=ALU.mult, op1=ALU.add)
                        ins.then_inc(dw_done.sem, 1)

            def pool_pairs(b):
                if not first(b):
                    dve.wait_ge(*fa_ready.before(b))
                for t in range(T):
                    dve.wait_ge(*relu_done.of(b, t + 1))
                    src = frames(t)
                    dve.scalar_tensor_tensor(out=pooled_h[:, t, :], in0=src[:, D:2 * D], scalar=0.0, in1=even[:, t, :],
                                             op0=ALU.max, op1=ALU.max).then_inc(pool_done.sem, 1)


            def spectrum_stats(b):
                if first(b):
                    dve.wait_ge(fft_in.sem, FFT)
                else:
                    dve.wait_ge(*hz_done.before(b))
                dve.wait_ge(*sines_done.of(b))
                dve.wait_ge(*y_ready.of(b))
                cosines = xb[0:P, 0, 0:T * KL].rearrange("p (t l) -> p t l", l=KL)
                dve.tensor_tensor(res[:, :, 0:KL], cosines, sines, ALU.add)
                dve.tensor_tensor(res[:, :, KL:D], cosines[:, :, KL - 2:0:-1], sines[:, :, KL - 2:0:-1], ALU.subtract)\
                   .then_inc(spec_done.sem, 1)
                dve.wait_ge(*spec_done.of(b))
                stats(res, ln1, bn1)

            def spectrum_center(b):
                aggregate(b, ln1, bn1, ag1)
                plus_eps(ln1, ve1)
                for t in range(T):
                    dve.scalar_tensor_tensor(out=res[:, t, :], in0=res[:, t, :], scalar=ln1[1][:, t, 0:1], in1=rows[:, 0, :],
                                             op0=ALU.subtract, op1=ALU.mult).then_inc(lnt_done.sem, 1)

            def spectrum_norm(b):
                dve.wait_ge(*rs1.of(b))
                dve.wait_ge(*lnt_done.of(b))
                for t in range(T):
                    dve.scalar_tensor_tensor(out=res[:, t, :], in0=res[:, t, :], scalar=ln1[3][:, t:t + 1], in1=rows[:, 1, :],
                                             op0=ALU.mult, op1=ALU.add).then_inc(h0_done.sem, 1)
                dve.wait_ge(*h0_done.of(b))
                stats(res, ln2, bn2)
                aggregate(b, ln2, bn2, ag2)
                plus_eps(ln2, ve2)

            def second_norm(b):
                dve.wait_ge(*rs2.of(b))
                if not first(b):
                    dve.wait_ge(*xhT_ready.before(b))
                for t in range(T):
                    dve.tensor_scalar(xh[:, t, :], res[:, t, :], ln2[1][:, t, 0:1], ln2[3][:, t:t + 1],
                                      ALU.subtract, ALU.mult).then_inc(xh_done.sem, 1)

            def front_input(b):
                for c in range(CT):
                    dve.wait_ge(*xhT_high.of(b, c + 1))
                    dve.tensor_tensor(xhT[:, 1, c, 0:N], xb[0:C, c, 0:N], xhT[:, 0, c, 0:N], ALU.subtract).then_inc(xhT_done.sem, 1)

            def token_norms(b):
                if first(b):
                    dve.tensor_tensor(head_mask[:], head_mask[:], temp[:].unsqueeze(1).to_broadcast([128, IT, H1]), ALU.mult)
                dve.wait_ge(*sq_done.of(b))
                dve.tensor_scalar(nrm[:], nrm[:], 1e-24, None, ALU.max).then_inc(rn1.sem, 1)
                dve.wait_ge(*rn1.of(b))
                dve.reciprocal(rnrm[:], nrm[:]).then_inc(rn2.sem, 1)
                dve.wait_ge(*rn2.of(b))
                dve.tensor_tensor(rhead[:], head_mask[:], rnrm[:].unsqueeze(2).to_broadcast([128, IT, H1]), ALU.mult)\
                   .then_inc(rhead_done.sem, 1)

            def token_max(b):
                dve.wait_ge(*lg_ready.of(b))
                dve.tensor_reduce(lgm[:, 0:1], xb[0:H1, 0, 0:N], AX.X, ALU.max, negate=True).then_inc(lmax_done.sem, 1)

            def token_softmax(b):
                dve.wait_ge(*lexp_done.of(b))
                dve.reciprocal(lgm[:, 2:3], lgm[:, 1:2]).then_inc(pi_steps.sem, 1)
                dve.wait_ge(*pi_steps.of(b, 1))
                dve.tensor_scalar(lgm[:, 3:4], lgm[:, 1:2], lgm[:, 2:3], 1e-8, ALU.mult, ALU.add).then_inc(pi_steps.sem, 1)
                dve.tensor_scalar(pi[:, 0:N], lg[:, 0:N], lgm[:, 2:3], None, ALU.mult).then_inc(pi_steps.sem, 1)
                dve.wait_ge(*pi_steps.of(b, 2))
                dve.reciprocal(pi[:, N:NE], lgm[:, 3:4]).then_inc(pi_steps.sem, 1)
                dve.wait_ge(*pi_steps.of(b, 4))
                if not first(b):
                    dve.wait_ge(*pib_ready.before(b))
                dve.tensor_copy(pi_parts[0:H1, :], pi[:]).then_inc(pi_steps.sem, 1)
                dve.wait_ge(*pi_steps.of(b, 5))
                dve.tensor_tensor(pi_parts[32:32 + H1, :], pi[:], pi_parts[0:H1, :], ALU.subtract).then_inc(pi_low_done.sem, 1)

            def token_products(b, j0, j1):
                for j in range(j0, j1):
                    dve.wait_ge(*pib_ready.of(b, j + 1))
                    dve.tensor_tensor(u[:, j, :], w_s[:, j, :], xb[:, j % 2, 0:NE], ALU.mult).then_inc(u_done.sem, 1)
                    if j > 0:
                        dots_of(b, j - 1)
                if j1 == IT:
                    dots_of(b, IT - 1)

            def dots_of(b, j):
                dve.wait_ge(*u_done.of(b, j + 1))
                dve.tensor_tensor_reduce(out=junk[:, j % 2, 0:N], in0=u[:, j, 0:N], in1=w_s[:, j, 0:N], scale=1.0, scalar=0.0,
                                         op0=ALU.mult, op1=ALU.add, accum_out=dots[:, j:j + 1]).then_inc(dots_done.sem, 1)

            def scaled_weights(b):
                if first(b):
                    dve.wait_ge(rest_in.sem, REST)
                dve.wait_ge(*dots_done.of(b))
                dve.tensor_tensor(natt[:], dots[:], u[:, :, N], ALU.mult).then_inc(att_steps.sem, 1)
                dve.wait_ge(*att_steps.of(b, 1))
                dve.tensor_scalar(natt[:], natt[:], -1.0, -1.0, ALU.mult, ALU.add).then_inc(att_steps.sem, 1)
                dve.wait_ge(*att_steps.of(b, 2))
                dve.reciprocal(natt[:], natt[:]).then_inc(att_steps.sem, 1)
                dve.wait_ge(*att_steps.of(b, 3))
                dve.tensor_tensor(w_oa[:, 3:IT], w_out[:, 3:IT], natt[:, 3:IT].unsqueeze(2).to_broadcast([128, IT - 3, D]), ALU.mult)\
                   .then_inc(woa_done.sem, 1)

            def third_norm(b):
                dve.wait_ge(*hb_done.of(b))
                for k, (t0, t1) in enumerate(((0, 2), (2, 3))):
                    dve.wait_ge(*o_ready.of(b, k + 1))
                    dve.tensor_tensor(res[:, t0:t1, :], xb[0:P, k, 0:D * (t1 - t0)].rearrange("p (t d) -> p t d", d=D),
                                      res[:, t0:t1, :], ALU.add).then_inc(h1_done.sem, 1)
                dve.wait_ge(*h1_done.of(b))
                stats(res, ln3, bn3)
                aggregate(b, ln3, bn3, ag3)
                var = ln3[1][:, :, 1]
                dve.tensor_scalar(ve34[:, 0, :], var, EPS, None, ALU.add)
                dve.tensor_scalar(ve34[:, 1, :], var, 1 + EPS, EPS * EPS, ALU.mult, ALU.add).then_inc(ve3.sem, 1)
                if not first(b):
                    dve.wait_ge(*ns_ready.before(b))
                for t in range(T):
                    dve.scalar_tensor_tensor(out=nr[:, t, 0:D], in0=res[:, t, :], scalar=ln3[1][:, t, 0:1], in1=rows[:, 3, :],
                                             op0=ALU.subtract, op1=ALU.mult).then_inc(nrt_done.sem, 1)

            def third_norm_end(b):
                dve.wait_ge(*rs3.of(b))
                for t in range(T):
                    dve.wait_ge(*nrt_done.of(b, t + 1))
                    dve.scalar_tensor_tensor(out=nr[:, t, 0:D], in0=nr[:, t, 0:D], scalar=rs34[:, 1, t:t + 1], in1=rows[:, 4, :],
                                             op0=ALU.mult, op1=ALU.add).then_inc(nr_done.sem, 1)

            def block_input(b):
                if not first(b):
                    dve.wait_ge(*h2_done.before(b))
                for t in range(T):
                    dve.tensor_scalar(zed[:, t, :], res[:, t, :], ln3[1][:, t, 0:1], rs34[:, 0, t:t + 1],
                                      ALU.subtract, ALU.mult).then_inc(z_done.sem, 1)

            def pooled_row(b):
                dve.wait_ge(*pwm_high.of(b))
                dve.tensor_tensor(w_mp[C:C + 1, 1, 1, :], w_m[C:C + 1, 1, :], w_mp[C:C + 1, 0, 1, :], ALU.subtract)\
                   .then_inc(pwm_low.sem, 1)

            def routed_input(b):
                dve.wait_ge(*nT_high.of(b))
                dve.tensor_tensor(nT[0:C, 1, :, 0:N], zb[0:C, 0:2, 0:N], nT[0:C, 0, :, 0:N], ALU.subtract).then_inc(nT_done.sem, 1)

            def score_row(b):
                dve.wait_ge(*sc_row_high.of(b))
                dve.tensor_tensor(nT[C:C + 1, 1, 1, 0:N], zb[C:C + 1, 2, 0:N], nT[C:C + 1, 0, 1, 0:N], ALU.subtract)\
                   .then_inc(sc_row_done.sem, 1)

            def scores(b):
                dve.wait_ge(*sexp_done.of(b))
                dve.tensor_scalar(sexp[:], sexp[:], 1.0, None, ALU.add).then_inc(sc_steps.sem, 1)
                dve.wait_ge(*sc_steps.of(b, 1))
                dve.reciprocal(nr[:, :, D], sexp[:]).then_inc(sc_steps.sem, 1)

            def ranks(b):
                dve.wait_ge(*sb_ready.of(b))
                if not first(b):
                    dve.wait_ge(*rk_ready.before(b))
                for t in range(T):
                    dve.scalar_tensor_tensor(out=less[:, t, tok(t)], in0=zb[0:P, 2, tok(t)], scalar=nr[:, t, D:D + 1], in1=later[:],
                                             op0=ALU.is_equal, op1=ALU.mult).then_inc(eq_done.sem, 1)
                for t in range(T):
                    if t > 0:
                        dve.tensor_scalar(less[:, t, 0:P * t], zb[0:P, 2, 0:P * t], nr[:, t, D:D + 1], None, ALU.is_gt)
                    if t < T - 1:
                        dve.tensor_scalar(less[:, t, P * t + P:N], zb[0:P, 2, P * t + P:N], nr[:, t, D:D + 1], None, ALU.is_ge)
                    dve.wait_ge(*eq_done.of(b, t + 1))
                    dve.scalar_tensor_tensor(out=less[:, t, tok(t)], in0=zb[0:P, 2, tok(t)], scalar=nr[:, t, D:D + 1],
                                             in1=less[:, t, tok(t)], op0=ALU.is_gt, op1=ALU.add).then_inc(less_done.sem, 1)

            def pooled_tokens(b):
                dve.wait_ge(*pl_ready.of(b))
                dve.tensor_scalar(pl_s[:], zb[0:C, 1, 2:3], 1e-6, None, ALU.add).then_inc(pl_steps.sem, 1)
                dve.wait_ge(*pl_steps.of(b, 1))
                dve.reciprocal(pl_r[:], pl_s[:]).then_inc(pl_steps.sem, 1)
                dve.wait_ge(*pl_steps.of(b, 2))
                dve.tensor_scalar(pl[:], zb[0:C, 1, 0:CT], pl_r[:], None, ALU.mult).then_inc(pl_steps.sem, 1)

            def slots(b):
                dve.wait_ge(*rk_ready.of(b))
                if not first(b):
                    dve.wait_ge(*mix_ready.before(b))
                dve.tensor_scalar(putT[:, 0:N], zb[0:Q, 3, 0:N], slot[:], None, ALU.is_equal).then_inc(putT_done.sem, 1)

            def queries(b):
                dve.wait_ge(*q_ready.of(b))
                if not first(b):
                    dve.wait_ge(*ql_ready.before(b))
                for c in range(CT):
                    dve.tensor_tensor(qb[:, c, :, :], zb[0:C, 3, Q * c:Q * c + Q].unsqueeze(1).to_broadcast([C, H1 // 2, Q]),
                                            q_mask[:].unsqueeze(2).to_broadcast([C, H1 // 2, Q]), ALU.mult).then_inc(qb_done.sem, 1)

            def attention_max(b, j):
                dve.wait_ge(*ql_ready.of(b, j + 1))
                if j == 0 and not first(b):
                    dve.wait_ge(*prob_done.before(b))
                dve.tensor_reduce(nmax[:, j:j + 1], zb[:, j % 2, 0:N], AX.X, ALU.max, negate=True).then_inc(qmax_done.sem, 1)

            def attention_sum(b):
                dve.wait_ge(*prob_done.of(b))
                dve.reciprocal(rsum_p[:], psum_p[:]).then_inc(rsum_done.sem, 1)

            def attention_context(b):
                dve.wait_ge(*rsum_done.of(b))
                dve.wait_ge(*pv_ready.of(b))
                if not first(b):
                    dve.wait_ge(*cxT_ready.before(b))
                cv = cx[:].rearrange("q (j a d) -> q j a d", j=IT, a=2)
                pv = zb[:, 0, 0:IT * 32].rearrange("q (j a d) -> q j a d", j=IT, a=2)
                dve.tensor_tensor(cv[:, :, 0, :], pv[0:Q, :, 0, :], rsum_p[0:Q, :].unsqueeze(2).to_broadcast([Q, IT, 16]), ALU.mult)
                dve.tensor_tensor(cv[:, :, 1, :], pv[Q:2 * Q, :, 1, :],
                                  rsum_p[Q:2 * Q, :].unsqueeze(2).to_broadcast([Q, IT, 16]), ALU.mult).then_inc(cx_done.sem, 1)

            def attention_out(b):
                dve.wait_ge(*ao_ready.of(b))
                dve.wait_ge(*ms_done.of(b))
                if not first(b):
                    dve.wait_ge(*mix_ready.before(b))
                dve.tensor_tensor(att[:], zb[0:Q, 1, 0:D], msel[:], ALU.subtract).then_inc(att_done.sem, 1)

            def fifth_norm(b):
                if not first(b):
                    dve.wait_ge(*h12_done.before(b))
                dve.wait_ge(*z_done.of(b))
                for k, (t0, t1) in enumerate(((0, 2), (2, 3))):
                    dve.wait_ge(*mix_ready.of(b, k + 1))
                    dve.tensor_tensor(h2[:, t0:t1, :], zb[0:P, 2 + k, 0:D * (t1 - t0)].rearrange("p (t d) -> p t d", d=D),
                                      zed[:, t0:t1, :], ALU.add).then_inc(h2_done.sem, 1)
                dve.wait_ge(*h2_done.of(b))
                stats(h2, ln5, bn5)
                aggregate(b, ln5, bn5, ag5)
                plus_eps(ln5, ve5)
                if not first(b):
                    dve.wait_ge(*n2T_ready.before(b))
                for t in range(T):
                    dve.scalar_tensor_tensor(out=n2[:, t, :], in0=h2[:, t, :], scalar=ln5[1][:, t, 0:1], in1=rows[:, 5, :],
                                             op0=ALU.subtract, op1=ALU.mult).then_inc(n2t_done.sem, 1)

            def fifth_norm_end(b):
                dve.wait_ge(*rs5.of(b))
                for t in range(T):
                    dve.wait_ge(*n2t_done.of(b, t + 1))
                    dve.scalar_tensor_tensor(out=n2[:, t, :], in0=n2[:, t, :], scalar=ln5[3][:, t:t + 1], in1=rows[:, 6, :],
                                             op0=ALU.mult, op1=ALU.add).then_inc(n2_done.sem, 1)

            def forward_input(b):
                dve.wait_ge(*n2T_high.of(b))
                dve.tensor_tensor(n2T[:, 1, :, 0:N], zb[0:C, 0:2, 0:N], n2T[:, 0, :, 0:N], ALU.subtract).then_inc(n2T_done.sem, 1)

            def result(b, i):
                if i == 0:
                    dve.wait_ge(*h12_done.of(b))
                t0, t1 = ((0, 2), (2, 3))[i]
                dve.wait_ge(*w2_ready.of(b, i + 1))
                dve.tensor_tensor(y_out[:, t0:t1, :], yb[0:P, i, 0:D * (t1 - t0)].rearrange("p (t d) -> p t d", d=D),
                                  res_f[:, t0:t1, :], ALU.add).then_inc(y_done.sem, 1)

            def step(p, q, r, w):
                front, middle, last = p is not None, q is not None, r is not None
                taps = ((0, 0), (0, 2), (2, 3), (3, 3), (3, 5), (5, 7)) if first(p) else ((0, 3), (3, 4), (4, 5), (5, 6), (6, 7), (7, 7))
                if front:
                    pool_pairs(p)
                if middle:
                    block_input(q)
                    routed_input(q)
                depthwise(w, *taps[0])
                if middle:
                    scores(q)
                    ranks(q)
                if front:
                    spectrum_stats(p)
                if middle:
                    slots(q)
                    pooled_tokens(q)
                if front:
                    spectrum_center(p)
                    spectrum_norm(p)
                if middle:
                    score_row(q)
                if front:
                    second_norm(p)
                if middle:
                    queries(q)
                if front:
                    front_input(p)
                if middle:
                    pooled_row(q)
                for j in range(IT):
                    if middle:
                        attention_max(q, j)
                    if j in (1, 3, 5):
                        depthwise(w, *taps[1 + j // 2])
                if front:
                    token_norms(p)
                    if first(p):
                        dve.tensor_copy(head_sel[:], head_sel32).then_inc(consts.sem, 1)
                depthwise(w, *taps[4])
                if front:
                    token_max(p)
                if middle:
                    attention_sum(q)
                if front:
                    token_softmax(p)
                    token_products(p, 0, 3)
                if middle:
                    attention_context(q)
                if front:
                    token_products(p, 3, 5)
                if middle:
                    attention_out(q)
                if front:
                    token_products(p, 5, 6)
                    scaled_weights(p)
                if middle:
                    fifth_norm(q)
                    fifth_norm_end(q)
                if last:
                    result(r, 0)
                    result(r, 1)
                depthwise(w, *taps[5])
                if front:
                    third_norm(p)
                if middle:
                    forward_input(q)
                if front:
                    third_norm_end(p)

            depthwise(0, 0, K)
            pipeline(dve, step)

        @block.gpsimd
        def _(pool):
            pool.memset(half3[:], -0.5).then_inc(consts.sem, 1)
            pool.wait_ge(consts.sem, FILLS)
            pool.wait_ge(fft_in.sem, FFT)
            pool.memset(xhT[:].bitcast(fp32), 0.0).then_inc(split.sem, 1)
            pool.memset(n2T[:].bitcast(fp32), 0.0).then_inc(split.sem, 1)
            pool.memset(nT[:].bitcast(fp32), 0.0).then_inc(split.sem, 1)
            pool.memset(w_v[:].bitcast(fp32), 0.0).then_inc(split.sem, 1)
            pool.wait_ge(split.sem, 4)
            pool.memset(nT[C:C + 1, 0, 0, :].bitcast(fp32), 1.0).then_inc(split.sem, 1)

            def split_weight(k, parts, weight):
                high, low = (parts[:, i, ..., 0:weight.shape[-1]] if len(weight.shape) == 3 else parts[:, i] for i in range(2))
                pool.tensor_copy(high, weight).then_inc(split.sem, 1)
                pool.wait_ge(split.sem, MEMSETS + 2 * k + 1)
                pool.tensor_tensor(low, weight, high, ALU.subtract).then_inc(split.sem, 1)

            def split_gelu(b, j0, j1):
                if b is None:
                    return
                for j in range(j0, j1):
                    pool.wait_ge(*gelu_high_done.of(b, j + 1))
                    pool.tensor_tensor(gelu_low[:, j, 0:N], gelu[:, j % 3, 0:N], gelu_high[:, j, 0:N], ALU.subtract)\
                        .then_inc(gelu_low_done.sem, 1)

            split_weight(0, w_qkv, w_qkv32)

            def power(b, out_, in_, ve, rs):
                pool.wait_ge(*ve.of(b))
                pool.tensor_tensor(out_[:], in_[:], half3[:] if len(in_.shape) == 3 else half3[:, 0, :], ALU.pow).then_inc(rs.sem, 1)

            def step(p, q, r, w):
                split_gelu(r, 0, 1)
                if p is not None:
                    power(p, ln1[3], ln1[2], ve1, rs1)
                split_gelu(r, 1, 3)
                if p is not None:
                    power(p, ln2[3], ln2[2], ve2, rs2)
                split_gelu(r, 3, IT)
                if p is not None:
                    pool.wait_ge(*xh_done.of(p))
                    pool.tensor_tensor(res[:], res[:], rows[:, 2:3, :].to_broadcast([P, T, D]), ALU.add).then_inc(hb_done.sem, 1)
                if first(p):
                    pool.wait_ge(rest_in.sem, REST)
                    pool.wait_ge(w_1_in.sem, 16)
                    split_weight(1, w_1, w_qkv32)
                    split_weight(2, w_2, w_2_32)
                    split_weight(3, w_k, w_k32)
                    split_weight(4, w_v, w_v32)
                    split_weight(5, w_mp, w_m[:])
                if q is not None:
                    power(q, ln5[3], ln5[2], ve5, rs5)
                if p is not None:
                    power(p, rs34, ve34, ve3, rs3)
                if q is not None:
                    pool.wait_ge(*h2_done.of(q))
                    pool.wait_ge(*hz_done.of(q))
                    if not first(q):
                        pool.wait_ge(*stored.before(q))
                    pool.tensor_tensor(res_f[:], res_q[:], h2[:], ALU.add).then_inc(h12_done.sem, 1)
                if p is not None:
                    pool.wait_ge(*h1_done.of(p))
                    if not first(p):
                        pool.wait_ge(*h12_done.before(p))
                    pool.tensor_tensor(res_q[:], res[:], rows[:, 7:8, :].to_broadcast([P, T, D]), ALU.add).then_inc(hz_done.sem, 1)

            pipeline(pool, step)

        @block.scalar
        def _(act):
            act.wait_ge(*x_ready.of(0))
            for dst, name in rests:
                act.dma_start(dst if isinstance(dst, bass.AP) else dst[:], dram[name]).then_inc(rest_in.sem, 16)

            def relu(b):
                if not first(b):
                    act.wait_ge(*xhT_ready.before(b))
                for t in range(T):
                    act.wait_ge(*pw_ready.of(b, t + 1))
                    src = frames(t)
                    act.activation(even[:, t, :], src[:, 0:D], ACT.Relu).then_inc(relu_done.sem, 1)

            def spectrum_parts(b):
                act.wait_ge(*fa_ready.of(b))
                if not first(b):
                    act.wait_ge(*o_ready.before(b))
                act.activation(fc[:, :, 0:KF], xb[0:C, :, 0:KF], ACT.Copy)
                act.activation(fs[:, :, 0:KF], xb[0:C, :, KF:2 * KF], ACT.Copy)
                act.activation(fc[:, :, KF:N], xb[0:C, :, KF - 1:0:-1], ACT.Copy)
                act.activation(fs[:, :, KF:N], xb[0:C, :, 2 * KF - 1:KF:-1], ACT.Copy, scale=-1.0).then_inc(fcs_done.sem, 1)

            def spectrum_sines(b):
                act.wait_ge(*y_ready.of(b, 1))
                act.activation(sines, xb[0:P, 1, 0:T * KL].rearrange("p (t l) -> p t l", l=KL), ACT.Copy).then_inc(sines_done.sem, 1)

            def front_input(b):
                act.wait_ge(*xhT_ready.of(b))
                if first(b):
                    act.wait_ge(split.sem, MEMSETS)
                else:
                    act.wait_ge(*qkv_ready.before(b))
                for c in range(CT):
                    act.activation(xhT[:, 0, c, 0:N], xb[0:C, c, 0:N], ACT.Copy).then_inc(xhT_high.sem, 1)
                if first(b):
                    act.wait_ge(consts.sem, FILLS)

            def squares(b, j):
                act.wait_ge(*qkv_ready.of(b, j + 1))
                if j == 0 and not first(b):
                    act.wait_ge(*dots_done.before(b))
                    act.wait_ge(*o_ready.before(b))
                act.activation(w_s[:, j, 0:N], xb[:, j % 2, 0:N], ACT.Copy)
                act.activation(w_sq[:, j, 0:N], xb[:, j % 2, 0:N], ACT.Square, accum_out=nrm[:, j:j + 1]).then_inc(sq_done.sem, 1)

            def token_exp(b):
                act.wait_ge(*lmax_done.of(b))
                act.activation(lg[:, 0:N], xb[0:H1, 0, 0:N], ACT.Exp, bias=lgm[:, 0:1], accum_out=lgm[:, 1:2]).then_inc(lexp_done.sem, 1)

            def scaled_weights(b):
                if first(b):
                    act.wait_ge(rest_in.sem, REST)
                act.wait_ge(*att_steps.of(b))
                for j in range(3):
                    ins = act.activation(w_oa[:, j, :], w_out[:, j, :], ACT.Copy, scale=natt[:, j:j + 1])
                ins.then_inc(woa_act_done.sem, 1)

            def routed_input(b):
                act.wait_ge(*nT_ready.of(b))
                if not first(b):
                    act.wait_ge(*mix_ready.before(b))
                else:
                    act.wait_ge(split.sem, SPLIT)
                act.activation(nT[0:C, 0, :, 0:N], zb[0:C, 0:2, 0:N], ACT.Copy).then_inc(nT_high.sem, 1)

            def keys_values(b):
                act.wait_ge(*k_ready.of(b))
                if not first(b):
                    act.wait_ge(*ql_ready.before(b))
                for c in range(CT):
                    ins = act.activation(kT[:, c, 0:N], zb[0:C, 2 + c, 0:N], ACT.Identity, bias=b_k[:, c:c + 1])
                ins.then_inc(kT_done.sem, 1)
                for k, (t0, t1) in enumerate(((0, 2), (2, 3))):
                    src = zb[0:P, k, 0:DV * (t1 - t0)].rearrange("p (t d) -> p t d", d=DV)
                    act.wait_ge(*v_ready.of(b, k + 1))
                    if k == 0 and not first(b):
                        act.wait_ge(*pv_ready.before(b))
                    act.activation(sexp[:, t0:t1], src[:, :, D], ACT.Exp, scale=-1.0).then_inc(sexp_done.sem, 1)
                for k, (t0, t1) in enumerate(((0, 2), (2, 3))):
                    src = zb[0:P, k, 0:DV * (t1 - t0)].rearrange("p (t d) -> p t d", d=DV)
                    act.activation(v[:, t0:t1, :], src[:, :, 0:D], ACT.Copy).then_inc(v_done.sem, 1)

            def score_row(b):
                act.wait_ge(*less_done.of(b))
                act.activation(nT[C:C + 1, 0, 1, 0:N], zb[C:C + 1, 2, 0:N], ACT.Copy).then_inc(sc_row_high.sem, 1)

            def pooled_row(b):
                act.wait_ge(*pwm_ready.of(b))
                if not first(b):
                    act.wait_ge(*pwm_low.before(b))
                act.activation(w_m[C:C + 1, 1, :], zb[0:1, 1, 64:64 + D], ACT.Copy).then_inc(pwm_done.sem, 1)
                act.wait_ge(*pwm_done.of(b))
                act.activation(w_mp[C:C + 1, 0, 1, :], w_m[C:C + 1, 1, :], ACT.Copy).then_inc(pwm_high.sem, 1)

            def slots(b):
                act.wait_ge(*put_ready.of(b))
                act.activation(put[:], zb[0:P, 0, 0:T * Q].rearrange("p (t q) -> p t q", q=Q), ACT.Copy).then_inc(put_done.sem, 1)

            def selected(b):
                act.wait_ge(*ns_ready.of(b))
                act.activation(nsT[0:C, 0, :], zb[0:C, 3, 0:Q], ACT.Copy)
                act.activation(nsT[:, 1, :], zb[0:C + 1, 3, Q:2 * Q], ACT.Copy).then_inc(ns_done.sem, 1)

            def selected_mix(b):
                act.wait_ge(*ms_ready.of(b))
                if not first(b):
                    act.wait_ge(*att_done.before(b))
                act.activation(msel[:], zb[0:Q, 1, 0:D], ACT.Copy).then_inc(ms_done.sem, 1)

            def exponentials(b, j):
                act.wait_ge(*qmax_done.of(b, j + 1))
                if j == 0 and first(b):
                    act.wait_ge(split.sem, SPLIT)
                elif j == 0:
                    act.wait_ge(*prT_ready.before(b))
                    act.wait_ge(*rsum_done.before(b))
                act.activation(probs[:, j, 0:N], zb[:, j % 2, 0:N], ACT.Exp, bias=nmax[:, j:j + 1],
                               accum_out=psum_p[:, j:j + 1]).then_inc(prob_done.sem, 1)

            def turned(b, j):
                act.wait_ge(*prT_ready.of(b, j + 1))
                act.activation(probsT[:, j, :, :], zb[0:P, 2 + j % 2, 0:T * 128].rearrange("p (t q) -> p t q", q=128),
                               ACT.Copy).then_inc(prT_done.sem, 1)

            def context(b):
                act.wait_ge(*cxT_ready.of(b))
                act.activation(cxT[0:C, :, :], zb[0:C, 0, 0:2 * Q].rearrange("p (c q) -> p c q", q=Q), ACT.Copy).then_inc(cxT_done.sem, 1)

            def forward_input(b):
                act.wait_ge(*n2T_ready.of(b))
                if first(b):
                    act.wait_ge(split.sem, MEMSETS)
                else:
                    act.wait_ge(*w1_ready.before(b))
                act.activation(n2T[:, 0, :, 0:N], zb[0:C, 0:2, 0:N], ACT.Copy).then_inc(n2T_high.sem, 1)

            def gelus(b, j):
                act.wait_ge(*w1_ready.of(b, j + 1))
                if j >= 3:
                    act.wait_ge(*gelu_low_done.of(b, j - 2))
                act.activation(gelu[:, j % 3, 0:N], yb[:, j % 2, 0:N], ACT.Gelu, bias=b_1[:, j:j + 1]).then_inc(gelu_done.sem, 1)
                if j == 0 and not first(b):
                    act.wait_ge(*w2_ready.before(b))
                act.wait_ge(*gelu_done.of(b, j + 1))
                act.activation(gelu_high[:, j, 0:N], gelu[:, j % 3, 0:N], ACT.Copy).then_inc(gelu_high_done.sem, 1)

            def step(p, q, r, w):
                front, middle, last = p is not None, q is not None, r is not None
                if front:
                    relu(p)
                if middle:
                    routed_input(q)
                if front:
                    spectrum_parts(p)
                if middle:
                    keys_values(q)
                if last and middle:
                    act.activation(table_hint[:], ones[0:1, 0:1], ACT.Gelu)
                if front:
                    spectrum_sines(p)
                if middle:
                    score_row(q)
                if last:
                    gelus(r, 0)
                    gelus(r, 1)
                    gelus(r, 2)
                if middle:
                    slots(q)
                    pooled_row(q)
                if last:
                    gelus(r, 3)
                if middle:
                    selected(q)
                if last:
                    gelus(r, 4)
                    gelus(r, 5)
                if middle:
                    selected_mix(q)
                if front:
                    front_input(p)
                if last and middle:
                    act.activation(table_hint[:], ones[0:1, 0:1], ACT.Exp)
                for j in range(IT):
                    if middle:
                        exponentials(q, j)
                    if front:
                        squares(p, j)
                    if middle:
                        if j:
                            turned(q, j - 1)
                if middle:
                    turned(q, IT - 1)
                if front:
                    token_exp(p)
                if middle:
                    context(q)
                if front:
                    scaled_weights(p)
                if middle:
                    forward_input(q)

            pipeline(act, step)

        @block.tensor
        def _(pe):
            mm = pe.matmul

            def transposes(src, dst):
                for c in range(CT):
                    for t in range(T):
                        ins = pe.transpose(dst[0:C, c, tok(t)], src[:, t, chan(c)], ident[0:P, 0:P])
                return ins

            pe.wait_ge(first_in.sem, FIRST)

            def split_product(o, a, b, start, stop):
                for k, l in ((0, 0), (0, 1), (1, 0)):
                    ins = mm(o, a[:, k], b[:, l], start=start and k + l == 0, stop=stop and k == 1)
                return ins

            def pointwise(b, q):
                pe.wait_ge(*dw_done.of(b))
                if not first(b):
                    pe.wait_ge(*h1_done.before(b))
                for t in range(T):
                    if t == 2 and q is not None and not first(q):
                        pe.wait_ge(*h2_done.before(q))
                    bank = frames(t)
                    for e in range(2):
                        f0 = 2 * P * t + e
                        o = bank[:, D * e:D * e + D]
                        mm(o, dw[0:C + 1, 0, f0:f0 + 2 * P - 1:2], w_pw[:, 0, :], start=True, stop=False)
                        ins = mm(o, dw[0:C, 1, f0:f0 + 2 * P - 1:2], w_pw[0:C, 1, :], start=False, stop=True)
                    ins.then_inc(pw_ready.sem, 1)

            def over_tokens(b):
                if first(b):
                    pe.wait_ge(fft_in.sem, FFT)
                pe.wait_ge(*pool_done.of(b))
                for c in range(CT):
                    for t in range(T):
                        ins = mm(xb[0:C, c, 0:2 * KF], pooled_h[:, t, chan(c)], dft_n[:, t, :], start=(t == 0), stop=(t == T - 1))
                ins.then_inc(fa_ready.sem, 1)

            def over_channels(b):
                pe.wait_ge(*fcs_done.of(b))
                for r, f in ((1, fs), (0, fc)):
                    for t in range(T):
                        for c in range(CT):
                            ins = mm(xb[0:P, r, KL * t:KL * t + KL], f[:, c, tok(t)], dft_d[:, r, c, :], start=(c == 0), stop=(c == 1))
                    ins.then_inc(y_ready.sem, 1)

            def front_input(b):
                pe.wait_ge(*xh_done.of(b))
                transposes(xh, xb).then_inc(xhT_ready.sem, 1)

            def qkv(b, j):
                if j == 0:
                    if first(b):
                        pe.wait_ge(split.sem, MEMSETS + 2)
                if j >= 2:
                    pe.wait_ge(*sq_done.of(b, j - 1))
                for c in range(CT):
                    if j == 0:
                        pe.wait_ge(*xhT_done.of(b, c + 1))
                    ins = split_product(xb[:, j % 2, 0:NE], w_qkv[:, :, c, 128 * j:128 * j + 128], xhT[:, :, c, :], c == 0, c == 1)
                ins.then_inc(qkv_ready.sem, 1)

            def token_logits(b):
                pe.wait_ge(*rhead_done.of(b))
                for j in range(IT):
                    ins = mm(xb[0:H1, 0, 0:N], rhead[:, j, :], w_sq[:, j, 0:N], start=(j == 0), stop=(j == IT - 1))
                ins.then_inc(lg_ready.sem, 1)

            def spread(b, j):
                if j == 0:
                    if first(b):
                        pe.wait_ge(consts.sem, SELECTORS)
                    pe.wait_ge(*pi_low_done.of(b))
                if j >= 2:
                    pe.wait_ge(*u_done.of(b, j - 1))
                mm(xb[:, j % 2, 0:NE], head_sel[:, j, :], pi_parts[:], start=True, stop=True).then_inc(pib_ready.sem, 1)

            def token_out(b):
                pe.wait_ge(*woa_done.of(b))
                pe.wait_ge(*woa_act_done.of(b))
                for t in range(T):
                    o = xb[0:P, t // 2, D * (t % 2):D * (t % 2) + D]
                    for j in range(IT):
                        ins = mm(o, u[:, j, tok(t)], w_oa[:, j, :], start=(j == 0), stop=(j == IT - 1))
                    if t:
                        ins.then_inc(o_ready.sem, 1)

            def routed_input(b):
                pe.wait_ge(*nr_done.of(b))
                if not first(b):
                    pe.wait_ge(*n2T_done.before(b))
                transposes(nr, zb).then_inc(nT_ready.sem, 1)

            def keys_values(b, p):
                if first(b):
                    pe.wait_ge(split.sem, SPLIT)
                pe.wait_ge(*nT_done.of(b))
                if p is not None:
                    pe.wait_ge(*pool_done.of(p))
                if not first(b):
                    pe.wait_ge(*h2_done.before(b))
                for k in range(CT):
                    for c in range(CT):
                        ins = split_product(zb[0:C, 2 + k, 0:NE], w_k[:, :, c, chan(k)], nT[0:C, :, c, :], c == 0, c == 1)
                ins.then_inc(k_ready.sem, 1)
                for t in range(T):
                    o = zb[0:P, t // 2, DV * (t % 2):DV * (t % 2) + DV]
                    split_product(o, nT[:, :, 0, tok(t)], w_v[:, :, 0, :], True, False)
                    ins = split_product(o, nT[0:C, :, 1, tok(t)], w_v[0:C, :, 1, :], False, True)
                    if t:
                        ins.then_inc(v_ready.sem, 1)

            def score_sums(b):
                pe.wait_ge(*kT_done.of(b))
                pe.wait_ge(*sc_steps.of(b))
                for t in range(T):
                    ins = pe.transpose(zb[0:P, 2, tok(t)], nr[:, t, D:D + 1].to_broadcast([P, P]), ident[0:P, 0:P])
                ins.then_inc(sb_ready.sem, 1)

            def pooled_sums(b):
                pe.wait_ge(*v_done.of(b))
                for c in range(CT + 1):
                    for t in range(T):
                        lhs = ones[:] if c == CT else nr[:, t, chan(c)]
                        ins = mm(zb[0:C, 1, c:c + 1], lhs, nr[:, t, D:D + 1], start=(t == 0), stop=(t == T - 1))
                ins.then_inc(pl_ready.sem, 1)

            def pooled_row(b):
                pe.wait_ge(*pl_steps.of(b))
                for c in range(CT):
                    ins = mm(zb[0:1, 1, 64:64 + D], pl[:, c:c + 1], w_m[0:C, c, :], start=(c == 0), stop=(c == 1))
                ins.then_inc(pwm_ready.sem, 1)

            def ranks(b):
                pe.wait_ge(*less_done.of(b))
                for t in range(T):
                    ins = mm(zb[0:Q, 3, 0:N], ones_bf[:], less[:, t, 0:N], start=(t == 0), stop=(t == T - 1))
                ins.then_inc(rk_ready.sem, 1)

            def slots(b):
                pe.wait_ge(*putT_done.of(b))
                for t in range(T):
                    ins = mm(zb[0:P, 0, Q * t:Q * t + Q], putT[:, tok(t)], ident[0:Q, 0:Q], start=True, stop=True)
                ins.then_inc(put_ready.sem, 1)

            def selected(b):
                pe.wait_ge(*put_done.of(b))
                for c in range(CT):
                    cols = chan(0) if c == 0 else slice(C, D + 1)
                    for t in range(T):
                        ins = mm(zb[0:C + c, 3, Q * c:Q * c + Q], nr[:, t, cols], put[:, t, :], start=(t == 0), stop=(t == T - 1))
                ins.then_inc(ns_ready.sem, 1)

            def selected_products(b):
                pe.wait_ge(*ns_done.of(b))
                for k in range(CT):
                    o = zb[0:C, 3, Q * k:Q * k + Q]
                    mm(o, w_q[:, 0, chan(k)], nsT[:, 0, :], start=True, stop=False)
                    ins = mm(o, w_q[0:C, 1, chan(k)], nsT[0:C, 1, :], start=False, stop=True)
                ins.then_inc(q_ready.sem, 1)
                pe.wait_ge(*pwm_done.of(b))
                for c in range(CT):
                    ins = mm(zb[0:Q, 1, 0:D], nsT[:, c, :], w_m[:, c, :], start=(c == 0), stop=(c == 1))
                ins.then_inc(ms_ready.sem, 1)

            def logits(b, j):
                if j in (0, 3):
                    pe.wait_ge(*qb_done.of(b, 1 + j // 3))
                if j == 1:
                    pe.wait_ge(*ms_done.of(b))
                if j >= 2:
                    pe.wait_ge(*prob_done.of(b, j - 1))
                c, i = divmod(j, 3)
                mm(zb[:, j % 2, 0:N], qb[:, c, 2 * i:2 * i + 2, :].rearrange("p h q -> p (h q)"), kT[:, c, 0:N],
                   start=True, stop=True).then_inc(ql_ready.sem, 1)

            def turn(b, j):
                if j == 0:
                    pe.wait_ge(*sc_row_done.of(b))
                if j >= 2:
                    pe.wait_ge(*prT_done.of(b, j - 1))
                pe.wait_ge(*prob_done.of(b, j + 1))
                for t in range(T):
                    ins = pe.transpose(zb[0:P, 2 + j % 2, 128 * t:128 * t + 128], probs[:, j, tok(t)], ident[:])
                ins.then_inc(prT_ready.sem, 1)

            def values(b, j):
                pe.wait_ge(*prT_done.of(b, j + 1))
                for t in range(T):
                    ins = mm(zb[:, 0, 32 * j:32 * j + 32], probsT[:, j, t, :], v[:, t, 32 * j:32 * j + 32],
                             start=(t == 0), stop=(t == T - 1))
                if j == IT - 1:
                    ins.then_inc(pv_ready.sem, 1)

            def context(b):
                pe.wait_ge(*cx_done.of(b))
                for c in range(CT):
                    ins = mm(zb[0:C, 0, Q * c:Q * c + Q], cx[:, chan(c)], ident[0:Q, 0:Q], start=True, stop=True)
                ins.then_inc(cxT_ready.sem, 1)

            def attention_out(b):
                pe.wait_ge(*cxT_done.of(b))
                mm(zb[0:Q, 1, 0:D], cxT[:, 0, :], w_o[:, 0, :], start=True, stop=False)
                mm(zb[0:Q, 1, 0:D], cxT[0:C, 1, :], w_o[0:C, 1, :], start=False, stop=True).then_inc(ao_ready.sem, 1)

            def mixed(b, t):
                if t == 0:
                    pe.wait_ge(*pwm_low.of(b))
                for c in range(CT):
                    split_product(zb[0:P, 2 + t // 2, D * (t % 2):D * (t % 2) + D], nT[:, :, c, tok(t)], w_mp[:, :, c, :], c == 0, False)

            def replaced(b, t):
                if t == 0:
                    pe.wait_ge(*att_done.of(b))
                ins = mm(zb[0:P, 2 + t // 2, D * (t % 2):D * (t % 2) + D], putT[:, tok(t)], att[:], start=False, stop=True)
                if t:
                    ins.then_inc(mix_ready.sem, 1)

            def forward_input(b):
                pe.wait_ge(*n2_done.of(b))
                transposes(n2, zb).then_inc(n2T_ready.sem, 1)

            def forward_up(b, j):
                if j == 0:
                    pe.wait_ge(*n2T_done.of(b))
                    if first(b):
                        pe.wait_ge(split.sem, SPLIT)
                    else:
                        pe.wait_ge(*y_done.before(b))
                if j >= 2:
                    pe.wait_ge(*gelu_done.of(b, j - 1))
                for c in range(CT):
                    ins = split_product(yb[:, j % 2, 0:NE], w_1[:, :, c, 128 * j:128 * j + 128], n2T[:, :, c, :], c == 0, c == 1)
                ins.then_inc(w1_ready.sem, 1)

            def forward_down(b, t, j):
                if t + j == 0:
                    pe.wait_ge(*gelu_low_done.of(b))
                    pe.wait_ge(*gelu_done.of(b))
                o = yb[0:P, t // 2, D * (t % 2):D * (t % 2) + D]
                for g, l in ((gelu_high, 0), (gelu_high, 1), (gelu_low, 0)):
                    ins = mm(o, g[:, j, tok(t)], w_2[:, l, j, :], start=(j == 0 and g is gelu_high and l == 0),
                             stop=(j == IT - 1 and g is gelu_low))
                if t and j == IT - 1:
                    ins.then_inc(w2_ready.sem, 1)

            def step(p, q, r, w):
                front, middle, last = p is not None, q is not None, r is not None
                if front:
                    pointwise(p, q)
                if last:
                    forward_up(r, 0)
                if middle:
                    routed_input(q)
                if front:
                    over_tokens(p)
                if middle:
                    keys_values(q, p)
                if last:
                    forward_up(r, 1)
                if middle:
                    score_sums(q)
                if front:
                    over_channels(p)
                if middle:
                    pooled_sums(q)
                    ranks(q)
                if last:
                    forward_up(r, 2)
                    forward_up(r, 3)
                if middle:
                    slots(q)
                    pooled_row(q)
                if last:
                    forward_up(r, 4)
                if middle:
                    selected(q)
                if last:
                    forward_up(r, 5)
                if middle:
                    selected_products(q)
                if front:
                    front_input(p)
                if middle:
                    logits(q, 0)
                    logits(q, 1)
                for j in range(IT):
                    if front:
                        qkv(p, j)
                    if middle:
                        if 1 <= j < IT - 1:
                            logits(q, j + 1)
                        if j:
                            turn(q, j - 1)
                if last:
                    for j in range(IT):
                        forward_down(r, 0, j)
                if front:
                    token_logits(p)
                if middle:
                    turn(q, IT - 1)
                for j in range(IT):
                    if middle:
                        values(q, j)
                    if last:
                        forward_down(r, 1, j)
                    if front and j >= 2:
                        spread(p, j - 2)
                if middle:
                    mixed(q, 0)
                    context(q)
                if front:
                    spread(p, 4)
                if middle:
                    mixed(q, 2)
                    attention_out(q)
                if front:
                    spread(p, 5)
                if last:
                    forward_down(r, 2, 0)
                    forward_down(r, 2, 1)
                if middle:
                    replaced(q, 0)
                    mixed(q, 1)
                    replaced(q, 1)
                    replaced(q, 2)
                if last:
                    for j in range(2, IT):
                        forward_down(r, 2, j)
                if front:
                    token_out(p)
                if middle:
                    forward_input(q)

            pipeline(pe, step)


def kernel(**inputs):
    import numpy as np
    import concourse.bacc as bacc
    from concourse.bass_utils import run_bass_kernel_spmd as run

    f = np.float32
    a = {k: np.asarray(v) for k, v in inputs.items()}

    def tiles(w, p):
        return np.ascontiguousarray(w.reshape(-1, p, w.shape[-1]).transpose(1, 0, 2))

    def with_row(w, row):
        extra = np.stack([row, np.zeros_like(row)])[None]
        return np.concatenate([tiles(w, C), extra], 0)

    x = np.zeros((B, CT, C, S + 6), f)
    x[:, :, :, 3:3 + S] = a["x"].transpose(0, 2, 1).reshape(B, CT, C, S)
    n, k, d = np.arange(N), np.arange(KF), np.arange(D)
    turn_n = 2 * np.pi * ((n[:, None] * k) % N) / N
    turn_d = 2 * np.pi * ((d[:, None] * np.arange(KL)) % D) / D
    p128, q = np.arange(128), np.arange(Q)
    head = 2 * np.arange(IT)[None, :] + (p128 // 64)[:, None]
    sel = np.zeros((64, IT, 128), f)
    for r in (0, 32):
        sel[r:r + H1] = (head.T[None] == np.arange(H1)[:, None, None])
    data = {
        "x": np.ascontiguousarray(x.transpose(0, 2, 1, 3)),
        "w_dw": tiles(np.concatenate([a["L0_tok_w_dw"][:, 0], a["L0_tok_b_dw"][:, None]], 1), C),
        "w_pw": with_row(a["L0_tok_w_pw"][:, :, 0].T, a["L0_tok_b_pw"]),
        "ones_row": np.ones((1, S), f),
        "dft_n": tiles(np.concatenate([np.cos(turn_n), np.sin(turn_n)], 1), P).astype(f),
        "dft_d": np.stack([tiles(np.cos(turn_d), C), tiles(-np.sin(turn_d), C)], 1).astype(f),
        "rows": np.broadcast_to(np.stack([a["L0_tok_gamma"], a["L0_tok_beta"], a["L0_attn_b_out"], a["L0_ffn_g1"], a["L0_ffn_b1"],
                                          a["L0_ffn_g2"], a["L0_ffn_b2"], a["L0_ffn_bf2"]]), (P, 8, D)),
        "ident": np.eye(128, dtype=f),
        "w_qkv": tiles(a["L0_attn_w_qkv"], C),
        "temp": np.broadcast_to(a["L0_attn_temp"][:, 0], (128, H1)),
        "head_mask": (head[:, :, None] == np.arange(H1)).astype(f),
        "head_sel": sel,
        "w_out": tiles(a["L0_attn_w_out"], 128),
        "w_k": tiles(a["L0_ffn_Wk"], C),
        "b_k": a["L0_ffn_bk"].reshape(CT, C).T,
        "w_v": with_row(np.concatenate([a["L0_ffn_Wv"], a["L0_ffn_Wr"][:, None]], 1),
                        np.concatenate([a["L0_ffn_bv"], a["L0_ffn_br"].reshape(1)])),
        "w_q": with_row(a["L0_ffn_Wq"], a["L0_ffn_bq"]),
        "w_o": with_row(a["L0_ffn_Wo"], a["L0_ffn_bo"]),
        "w_m": with_row(a["L0_ffn_Wm"], a["L0_ffn_bm"]),
        "q_mask": 0.25 * (np.arange(C)[:, None] // 16 == np.arange(H1 // 2)).astype(f),
        "later": np.triu(np.ones((P, P), f), 1),
        "slot": np.where(q < SEL, q, -1).astype(f)[:, None],
        "w_1": tiles(a["L0_ffn_W1"], C),
        "b_1": a["L0_ffn_bf1"].reshape(IT, 128).T,
        "w_2": tiles(a["L0_ffn_W2"], 128),
        "ones_q": np.ones((1, Q), f), "ones_q2": np.ones((1, Q), f),
    }
    nc = bacc.Bacc("TRN2", target_bir_lowering=False, num_devices=1)
    arrays, dram = {}, {}
    for name, value in data.items():
        value = np.ascontiguousarray(value)
        assert value.dtype == f, name
        arrays[f"in_{name}"] = value
        dram[name] = nc.dram_tensor(f"in_{name}", value.shape, mybir.dt.float32, kind="ExternalInput").ap()
    out = nc.dram_tensor("out_0", (B, N, D), mybir.dt.float32, kind="ExternalOutput").ap()
    audio_tower(nc, dram, out)
    result = run(nc, [arrays], core_ids=[0])
    return result.results[0]["out_0"]
```
